# Optimizing a Trainium2 kernel written in Bass

```python
import numpy as np
import jax
import jax.numpy as jnp

def _softmax(x, axis=-1):
    return jax.nn.softmax(x, axis=axis)

def _gelu(x):
    return jax.nn.gelu(x, approximate=True)

def _silu(x):
    return jax.nn.silu(x)

def _sigmoid(x):
    return jax.nn.sigmoid(x)

def _layernorm(x, axis=-1, eps=1e-05):
    m = jnp.mean(x, axis=axis, keepdims=True)
    v = jnp.var(x, axis=axis, keepdims=True)
    return (x - m) / jnp.sqrt(v + eps)

def _scatter_add(tgt, idx, src, axis=0):
    return tgt.at[idx].add(src)

def _segment_sum(src, seg, n):
    return jax.ops.segment_sum(src, seg, n)
kernel_name = 'mk_gnn_preln_d1_gnn_r32_ada01b'

def setup_inputs(seed: int=0):
    np.random.seed(seed)
    _w = jnp.asarray

    def _rec_inputs():
        import jax
        import jax.numpy as jnp
        _gk = jax.random.key(seed)
        x = -0.0002117 + 1 * jax.random.normal(jax.random.fold_in(_gk, 1), (50000, 512), jnp.float32)
        _s = jax.random.randint(jax.random.fold_in(_gk, 2), (12500,), 0, 50000, jnp.int32)
        _d = jax.random.randint(jax.random.fold_in(_gk, 3), (12500,), 0, 50000, jnp.int32)
        _loop = jnp.arange(50000, dtype=jnp.int32)
        src = jnp.concatenate([_s, _d, _loop])
        dst = jnp.concatenate([_d, _s, _loop])
        _o = jnp.argsort(dst, stable=True)
        src = src[_o]
        dst = dst[_o]
        return (x, src, dst)
    x, src, dst = _rec_inputs()

    def _L0_gnn_setup():
        import jax, jax.numpy as jnp
        import numpy as np
        N_NODES = 50000
        key = jax.random.key(seed)
        ks = jax.random.split(key, 5)
        d_in, d_out = (512, 512)
        n_edges = 25000
        x = jax.random.normal(ks[0], (N_NODES, d_in), dtype=jnp.float32)
        edge_index = jax.random.randint(ks[1], (2, n_edges), 0, N_NODES, dtype=jnp.int64)
        s = 1.0 / np.sqrt(d_in)
        W_l = jax.random.uniform(ks[2], (d_out, d_in), dtype=jnp.float32, minval=-s, maxval=s)
        b_l = jax.random.uniform(ks[3], (d_out,), dtype=jnp.float32, minval=-s, maxval=s)
        W_r = jax.random.uniform(ks[4], (d_out, d_in), dtype=jnp.float32, minval=-s, maxval=s)
        return {'x': x, 'edge_index': edge_index, 'W_l': W_l, 'b_l': b_l, 'W_r': W_r}
    _L0_gnn_all = _L0_gnn_setup()
    _L0_gnn_in = {k: v for k, v in _L0_gnn_all.items() if k in ('W_l', 'b_l', 'W_r')}
    del _L0_gnn_all
    return {'x': x, 'src': src, 'dst': dst, 'L0_gnn_W_l': _L0_gnn_in['W_l'], 'L0_gnn_b_l': _L0_gnn_in['b_l'], 'L0_gnn_W_r': _L0_gnn_in['W_r']}

def reference(x, src, dst, L0_gnn_W_l, L0_gnn_b_l, L0_gnn_W_r):
    import jax
    import jax.numpy as jnp

    def _L0_gnn_ref(x, edge_index, W_l, b_l, W_r):
        import jax, jax.numpy as jnp
        import numpy as np
        N_NODES = 50000
        x_l = x @ W_l.T + b_l
        src, dst = (edge_index[0], edge_index[1])
        agg = jax.ops.segment_sum(x_l[src], dst, num_segments=N_NODES)
        deg = jax.ops.segment_sum(jnp.ones_like(src, dtype=x.dtype), dst, num_segments=N_NODES)
        out_l = agg / jnp.maximum(deg, 1.0)[:, None]
        out_r = x @ W_r.T
        return out_l + out_r
    edge_index = jnp.stack([src, dst])
    h = jnp.maximum(_layernorm(x, axis=-1), 0.0)
    x = x + _L0_gnn_ref(h, edge_index, L0_gnn_W_l, L0_gnn_b_l, L0_gnn_W_r)
    return x

_drawn_inputs = setup_inputs


def setup_inputs(seed=0):
    import zlib

    import numpy as np

    out = dict(_drawn_inputs(seed))
    spreads = {}
    factors = {'L0_gnn_b_l': 2.689}
    for name, (base, spread) in spreads.items():
        noise = np.random.default_rng([zlib.crc32(name.encode()), seed]).standard_normal(out[name].shape)
        drawn = base * np.exp(spread * noise) if base else spread * noise
        out[name] = jnp.asarray(drawn.astype(out[name].dtype))
    for name, factor in factors.items():
        out[name] = (out[name] * factor).astype(out[name].dtype)
    return out
```

```python
from contextlib import ExitStack

import concourse.bass as bass
from concourse import mybir

P = 128
WINDOW = 3
SUB = 32
UNROLL = 6
FAR = float(1 << 17)
SCALE = 256.0
EPS = 1e-5

fp32, fp16, bf16, i32 = mybir.dt.float32, mybir.dt.float16, mybir.dt.bfloat16, mybir.dt.int32
ALU = mybir.AluOpType
ACT = mybir.ActivationFunctionType
AX = mybir.AxisListType
RMAX = bass.bass_isa.ReduceOp.max


class Shared:
    pass


class Tile:

    def __init__(self, turn, c):
        self.turn, self.c = turn, c
        self.index = turn * UNROLL + c
        self.static = isinstance(turn, int)

    def slot(self, depth):
        return self.c % depth

    def nth(self, depth):
        return self.turn * (UNROLL // depth) + self.c // depth + 1

    def exists(self, tiles):
        return not self.static or 0 <= self.index < tiles


def after(engine, semaphore, tile, lag=0):
    value = tile.index - lag + 1
    if tile.static and value <= 0:
        return
    engine.wait_ge(semaphore, value)


def gnn_kernel(nc, x, src, dst, w_l, b_l, w_r, out):
    N, D = x.shape
    E = src.shape[0]
    FC = D // P
    TILES = -(-N // P)
    LAST_BASE = N - P
    LAST_NEW = N - (TILES - 1) * P
    CHUNKS = -(-E // P)
    EG = -(-CHUNKS // P)
    COLS = EG * P
    NSUB = P // SUB
    ROW = EG * NSUB * P
    TG = -(-TILES // P)
    TCOLS = TG * P

    ctx = ExitStack()
    with ctx:
        def sb(name, shape, dt):
            return ctx.enter_context(nc.sbuf_tensor(name, shape, dt))

        ident = sb("ident", [P, P], fp32)
        ident16 = sb("ident16", [P, P], fp16)
        ones = sb("ones", [P, P], fp32)
        ones16 = sb("ones16", [P, P], fp16)
        upper = sb("upper", [P, P], fp16)
        from0 = sb("from0", [P, P], fp16)
        from1 = sb("from1", [P, P], fp16)
        weights = sb("weights", [P, 2, 2, FC, D], fp16)
        bias3 = sb("bias3", [P, D], bf16)
        fold = sb("fold", [P, 1], fp32)
        table = sb("table", [P, COLS + WINDOW, 6], fp32)
        src_of = sb("src_of", [P, COLS], i32)
        base_of = sb("base_of", [P, TCOLS], fp32)
        tinfo = sb("tinfo", [P, 4, TCOLS], i32)
        n_general = sb("n_general", [P, 1], i32)

        banks = [ctx.enter_context(nc.psum_tensor(f"bank{i}", [P, 512], fp32)) for i in range(8)]

        s = Shared()
        s.x, s.src, s.dst, s.w_l, s.b_l, s.w_r, s.out = x, src, dst, w_l, b_l, w_r, out
        (s.N, s.D, s.E, s.FC, s.TILES, s.LAST_BASE, s.LAST_NEW, s.EG, s.COLS, s.NSUB, s.ROW, s.TG, s.TCOLS) = (
            N, D, E, FC, TILES, LAST_BASE, LAST_NEW, EG, COLS, NSUB, ROW, TG, TCOLS)
        (s.ident, s.ident16, s.ones, s.ones16, s.upper, s.from0, s.from1) = (
            ident, ident16, ones, ones16, upper, from0, from1)
        (s.weights, s.bias3, s.fold, s.table, s.src_of, s.base_of, s.tinfo, s.n_general, s.banks) = (
            weights, bias3, fold, table, src_of, base_of, tinfo, n_general, banks)
        prepare(nc, s)
        fast(nc, s)
        general(nc, s)


def prepare(nc, s):
    D, E, FC, TILES, EG, COLS = s.D, s.E, s.FC, s.TILES, s.EG, s.COLS
    NSUB, ROW, TG, TCOLS, LAST_BASE = s.NSUB, s.ROW, s.TG, s.TCOLS, s.LAST_BASE
    ident, ident16, ones, ones16, upper, from0, from1 = s.ident, s.ident16, s.ones, s.ones16, s.upper, s.from0, s.from1
    weights, bias3, fold, table, src_of = s.weights, s.bias3, s.fold, s.table, s.src_of
    base_of, tinfo, n_general, banks = s.base_of, s.tinfo, s.n_general, s.banks
    with ExitStack() as ctx:
        def sb(name, shape, dt):
            return ctx.enter_context(nc.sbuf_tensor(name, shape, dt))

        def sem(name):
            return ctx.enter_context(nc.semaphore(name))

        raw_w = sb("raw_w", [P, 2, FC, D], fp32)
        raw_b = sb("raw_b", [P, D], fp32)
        part_b = sb("part_b", [P, 3, D], bf16)
        raw_dst = sb("raw_dst", [P, EG, P], i32)
        raw_src = sb("raw_src", [P, EG, P], i32)
        cut = sb("cut", [P, 2, EG, P], i32)
        edge = sb("edge", [P, 4, EG, P], fp32)
        subs = sb("subs", [P, 3, EG * NSUB], fp32)
        diag = sb("diag", [P, 2, 4, P], fp32)
        rows = sb("rows", [P, 3, ROW], fp32)
        end_id = sb("end_id", [P, ROW], fp32)
        rev_id = sb("rev_id", [P, ROW], fp32)
        meet = sb("meet", [P, ROW], fp32)
        scrap = sb("scrap", [P, ROW], fp32)
        base_col = sb("base_col", [P, TG, 2], fp32)
        found = sb("found", [P, TG, 3], fp32)
        info = sb("info", [P, 4, TG], fp32)
        wmax = sb("wmax", [P, 4], fp32)
        wint = sb("wint", [P, 2], i32)
        wscale = sb("wscale", [P, 1], fp32)
        spread = sb("spread", [P, TG], fp32)

        w_in, b_in, e_in = sem("w_in"), sem("b_in"), sem("e_in")
        e_filled = sem("e_filled")
        pool_done, consts = sem("pool_done"), sem("consts")
        wmax_ready, wmax_shared = sem("wmax_ready"), sem("wmax_shared")
        dve_done = sem("dve_done")
        w_turned, w_taken = sem("w_turned"), sem("w_taken")
        edge_ready, edge_turned, edge_taken = sem("edge_ready"), sem("edge_turned"), sem("edge_taken")
        diag_ready, row_ready, row_taken = sem("diag_ready"), sem("row_ready"), sem("row_taken")

        full, rest = E // P, E % P
        edge_loads = []
        for raw, flat in ((raw_dst, s.dst), (raw_src, s.src)):
            for g in range(EG):
                n = min(P, full - g * P)
                if n > 0:
                    edge_loads.append((raw[0:n, g, :], flat[g * P * P:(g * P + n) * P].rearrange("(q e) -> q e", e=P)))
            if rest:
                q = full % P
                edge_loads.append((raw[q:q + 1, full // P, 0:rest], flat[full * P:E].rearrange("(a e) -> a e", a=1)))

        with nc.Block(name="prepare") as block:
            @block.sync
            def _(sp):
                sp.dma_start(raw_w[:, 0, :, :], s.w_r.rearrange("(o p) f -> p o f", p=P)).then_inc(w_in, 16)
                sp.dma_start(raw_w[:, 1, :, :], s.w_l.rearrange("(o p) f -> p o f", p=P)).then_inc(w_in, 16)
                sp.dma_start(raw_b[:, :], s.b_l.rearrange("(a n) -> a n", a=1).broadcast_to([P, D])).then_inc(b_in, 16)
                sp.wait_ge(e_filled, 2)
                for to, frm in edge_loads:
                    sp.dma_start(to, frm).then_inc(e_in, 16)

            @block.gpsimd
            def _(pool):
                step = [0]

                def link(ins):
                    step[0] += 1
                    ins.then_inc(pool_done, 1)
                    pool.wait_ge(pool_done, step[0])

                pool.memset(raw_dst[:, :, :], 1 << 17).then_inc(e_filled, 1)
                pool.memset(raw_src[:, :, :], 0).then_inc(e_filled, 1)
                pool.memset(ones[:, :], 1.0)
                pool.memset(ones16[:, :], 1.0)
                link(pool.memset(ident[:, :], 0.0))
                link(pool.affine_select(out=ident[:, :], in_=ident[:, :], compare_op=ALU.not_equal, fill=1.0,
                                        base=0, pattern=[[-1, P]], channel_multiplier=1))
                link(pool.memset(ident16[:, :], 0.0))
                link(pool.affine_select(out=ident16[:, :], in_=ident16[:, :], compare_op=ALU.not_equal, fill=1.0,
                                        base=0, pattern=[[-1, P]], channel_multiplier=1))
                link(pool.memset(upper[:, :], 1.0))
                pool.affine_select(out=upper[:, :], in_=upper[:, :], compare_op=ALU.is_gt, fill=0.0,
                                   base=0, pattern=[[1, P]], channel_multiplier=-1)
                pool.iota(from0[:, :], pattern=[[1, P]], base=0, channel_multiplier=0,
                          allow_small_or_imprecise_dtypes=True)
                pool.iota(from1[:, :], pattern=[[1, P]], base=1, channel_multiplier=0,
                          allow_small_or_imprecise_dtypes=True)
                pool.iota(base_of[:, :], pattern=[[P, TCOLS]], base=0, channel_multiplier=0,
                          allow_small_or_imprecise_dtypes=True)
                pool.iota(base_col[:, :, 0], pattern=[[P * P, TG]], base=0, channel_multiplier=P,
                          allow_small_or_imprecise_dtypes=True)
                pool.iota(end_id[:, :], pattern=[[P, EG], [0, NSUB], [1, P]], base=1, channel_multiplier=0,
                          allow_small_or_imprecise_dtypes=True)
                link(pool.memset(table[:, COLS:COLS + WINDOW, :], 0.0))
                link(pool.memset(table[:, COLS:COLS + WINDOW, 0], FAR))
                pool.memset(table[:, :, 4], 1.0).then_inc(consts, 1)
                pool.wait_ge(wmax_ready, 1)
                pool.partition_all_reduce(wmax[:, 1:2], wmax[:, 0:1], P, RMAX)\
                    .then_inc(wmax_shared, 1)

            @block.vector
            def _(dve):
                step = [0]

                def link(ins):
                    step[0] += 1
                    ins.then_inc(dve_done, 1)
                    dve.wait_ge(dve_done, step[0])

                dve.wait_ge(w_in, 32)
                dve.tensor_reduce(wmax[:, 0:1], raw_w[:, :, :, :], AX.XYZ, ALU.max, apply_absolute_value=True)\
                    .then_inc(wmax_ready, 1)

                dve.wait_ge(consts, 1)
                dve.wait_ge(e_in, 16 * len(edge_loads))
                dve.tensor_copy(edge[:, 0, :, :], raw_dst[:, :, :])
                link(dve.tensor_copy(edge[:, 2, :, :], raw_src[:, :, :]))
                link(dve.tensor_tensor(edge[:, 1, :, :], edge[:, 0, :, :], edge[:, 2, :, :], ALU.not_equal))
                dve.tensor_scalar(cut[:, 0, :, :], raw_src[:, :, :], 8, None, ALU.logical_shift_right)
                link(dve.tensor_scalar(cut[:, 1, :, :], raw_src[:, :, :], 255, None, ALU.bitwise_and))
                dve.tensor_scalar(edge[:, 2, :, :], cut[:, 0, :, :], -512.0, None, ALU.add)
                dve.tensor_copy(edge[:, 3, :, :], cut[:, 1, :, :]).then_inc(edge_ready, 1)
                for g in range(EG):
                    dve.wait_ge(edge_turned, g + 1)
                    dve.tensor_copy(table[:, g * P:(g + 1) * P, 0:4],
                                    banks[2 + g % 2].rearrange("p (k q) -> p q k", k=4)).then_inc(edge_taken, 1)
                dve.wait_ge(edge_taken, EG)
                dve.tensor_scalar(table[:, :, 5], table[:, :, 1], -1.0, 1.0, ALU.mult, ALU.add)
                link(dve.tensor_scalar(scrap[:, 0:COLS], table[:, 0:COLS, 2], 512.0, 256.0, ALU.add, ALU.mult))
                dve.tensor_tensor(src_of[:, :], scrap[:, 0:COLS], table[:, 0:COLS, 3], ALU.add)

                by_sub = edge[:, :, :, :].rearrange("p k g (s e) -> p k (g s) e", e=SUB)
                dve.tensor_reduce(subs[:, 0, :], by_sub[:, 0], AX.X, ALU.min)
                dve.tensor_reduce(subs[:, 1, :], by_sub[:, 0], AX.X, ALU.max)
                link(dve.tensor_reduce(subs[:, 2, :], by_sub[:, 1], AX.X, ALU.add))
                dve.tensor_scalar(base_of[:, :], base_of[:, :], float(LAST_BASE), None, ALU.min)
                link(dve.tensor_scalar(base_col[:, :, 0], base_col[:, :, 0], float(LAST_BASE), None, ALU.min))
                dve.tensor_scalar(base_col[:, :, 1], base_col[:, :, 0], float(P), None, ALU.add)
                link(dve.tensor_scalar(rev_id[:, :], end_id[:, :], -1.0, float(COLS + 1), ALU.mult, ALU.add))

                turns = 0

                def row_turn(columns, take):
                    nonlocal turns
                    if turns >= 2:
                        dve.wait_ge(row_ready, turns - 1)
                    for k, column in enumerate(columns):
                        ins = dve.tensor_scalar(diag[:, turns % 2, k, :], ident[:, :], column, None, ALU.mult)
                    ins.then_inc(diag_ready, 1)
                    dve.wait_ge(row_ready, turns + 1)
                    take(banks[turns % 2]).then_inc(row_taken, 1)
                    turns += 1

                for k in range(3):
                    for c in range(0, EG * NSUB, 4):
                        row_turn([subs[:, k, c + i:c + i + 1] for i in range(4)],
                                 lambda bank: dve.tensor_copy(rows[:, k, c * P:(c + 4) * P], bank[:, :]))
                link(dve.memset(found[:, :, :], 0.0))

                for g in range(TG):
                    link(dve.tensor_scalar(meet[:, :], rows[:, 1, :], base_col[:, g, 0:1], None, ALU.is_ge))
                    link(dve.scalar_tensor_tensor(meet[:, :], rows[:, 0, :], base_col[:, g, 1:2], meet[:, :],
                                                  ALU.is_lt, ALU.mult))
                    for k, (weight, op) in enumerate(((rev_id[:, :], ALU.max), (end_id[:, :], ALU.max),
                                                      (rows[:, 2, :], ALU.add))):
                        link(dve.tensor_tensor_reduce(out=scrap[:, :], in0=meet[:, :], in1=weight, scale=1.0,
                                                      scalar=0.0, op0=ALU.mult, op1=op,
                                                      accum_out=found[:, g, k:k + 1]))
                dve.tensor_scalar(info[:, 0, :], found[:, :, 0], -1.0, float(COLS), ALU.mult, ALU.add)
                dve.tensor_copy(info[:, 1, :], found[:, :, 1])
                dve.tensor_copy(info[:, 3, :], base_col[:, :, 0])
                link(dve.tensor_scalar(info[:, 2, :], found[:, :, 2], float(P), None, ALU.is_gt))
                link(dve.tensor_tensor(spread[:, :], info[:, 1, :], info[:, 0, :], ALU.subtract))
                link(dve.scalar_tensor_tensor(info[:, 2, :], spread[:, :], float(WINDOW), info[:, 2, :],
                                              ALU.is_gt, ALU.max))
                for k in range(4):
                    for c in range(0, TG, 4):
                        w = min(4, TG - c)
                        row_turn([info[:, k, c + i:c + i + 1] for i in range(w)],
                                 lambda bank: dve.tensor_copy(tinfo[:, k, c * P:(c + w) * P], bank[:, 0:w * P]))
                link(dve.memset(spread[:, 0:1], 0.0))
                link(dve.tensor_reduce(spread[:, 0:1], tinfo[:, 2, 0:TILES], AX.X, ALU.add))
                link(dve.tensor_copy(n_general[:, :], spread[:, 0:1]))

                dve.wait_ge(wmax_shared, 1)
                link(dve.tensor_scalar(wint[:, 0:1], wmax[:, 1:2].bitcast(i32), 0x7F800000, None, ALU.bitwise_and))
                link(dve.tensor_scalar(wint[:, 0:1], wint[:, 0:1], float(32 << 23), None, ALU.max))
                link(dve.tensor_scalar(wint[:, 1:2], wint[:, 0:1], -1.0, float((254 + 8) << 23), ALU.mult, ALU.add))
                link(dve.tensor_copy(wscale[:, :], wint[:, 1:2].bitcast(fp32)))
                link(dve.tensor_scalar(wint[:, 0:1], wint[:, 0:1], float(16 << 23), None, ALU.subtract))
                link(dve.tensor_copy(fold[:, :], wint[:, 0:1].bitcast(fp32)))
                for n in range(2 * FC):
                    k, f = divmod(n, FC)
                    dve.wait_ge(w_turned, n + 1)
                    bank = banks[4 + n % 4]
                    link(dve.tensor_scalar(weights[:, k, 0, f, :], bank[:, :], wscale[:, :], None, ALU.mult))
                    dve.scalar_tensor_tensor(weights[:, k, 1, f, :], bank[:, :], wscale[:, :],
                                             weights[:, k, 0, f, :], ALU.mult, ALU.subtract).then_inc(w_taken, 1)
                dve.wait_ge(b_in, 16)
                link(dve.tensor_scalar(raw_b[:, :], raw_b[:, :], wscale[:, :], SCALE, ALU.mult, ALU.mult))
                for k in range(3):
                    link(dve.tensor_copy(part_b[:, k, :], raw_b[:, :]))
                    link(dve.tensor_tensor(raw_b[:, :], raw_b[:, :], part_b[:, k, :], ALU.subtract))
                link(dve.tensor_scalar(bias3[:, :], part_b[:, 0, :], ident[:, 0:1], None, ALU.mult))
                for k in range(1, 3):
                    link(dve.scalar_tensor_tensor(bias3[:, :], part_b[:, k, :], ident[:, k:k + 1], bias3[:, :],
                                                  ALU.mult, ALU.add))

            @block.tensor
            def _(pe):
                pe.wait_ge(consts, 1)
                pe.wait_ge(w_in, 32)
                pe.wait_ge(edge_ready, 1)
                for g in range(EG):
                    if g >= 2:
                        pe.wait_ge(edge_taken, g - 1)
                    for k in range(4):
                        last = pe.transpose(banks[2 + g % 2][:, k * P:(k + 1) * P], edge[:, k, g, :], ident[:, :])
                    last.then_inc(edge_turned, 1)
                widths = [4] * (3 * EG * NSUB // 4) + 4 * [min(4, TG - c) for c in range(0, TG, 4)]
                for n, width in enumerate(widths):
                    pe.wait_ge(diag_ready, n + 1)
                    if n >= 2:
                        pe.wait_ge(row_taken, n - 1)
                    pe.matmul(banks[n % 2][:, 0:width * P], ones[:, :], diag[:, n % 2, 0:width, :],
                              start=True, stop=True).then_inc(row_ready, 1)
                for n in range(2 * FC):
                    if n >= 4:
                        pe.wait_ge(w_taken, n - 3)
                    k, f = divmod(n, FC)
                    for o in range(FC):
                        last = pe.transpose(banks[4 + n % 4][:, o * P:(o + 1) * P],
                                            raw_w[:, k, o, f * P:(f + 1) * P], ident[:, :])
                    last.then_inc(w_turned, 1)


def fast(nc, s):
    x, out, D, FC, TILES = s.x, s.out, s.D, s.FC, s.TILES
    ident, ident16, ones16, upper, from0, from1 = s.ident, s.ident16, s.ones16, s.upper, s.from0, s.from1
    weights, bias3, fold, table, base_of, tinfo, banks = s.weights, s.bias3, s.fold, s.table, s.base_of, s.tinfo, s.banks
    LONG, MID, SHORT = 6, 3, 2
    with ExitStack() as ctx:
        def sb(name, shape, dt):
            return ctx.enter_context(nc.sbuf_tensor(name, shape, dt))

        def sem(name):
            return ctx.enter_context(nc.semaphore(name))

        own = sb("own", [P, LONG, D], fp32)
        far = sb("far", [P, LONG, D], fp32)
        result = sb("result", [P, MID, D], fp32)
        window = sb("window", [P, LONG, WINDOW, 6], fp32)
        local = sb("local", [P, LONG, WINDOW], fp32)
        begun = sb("begun", [P, LONG, WINDOW], fp32)
        sent = sb("sent", [P, LONG, WINDOW], fp16)
        cargo = sb("cargo", [P, LONG, WINDOW, 5], fp16)
        place = sb("place", [P, LONG, WINDOW], fp32)
        to_slot = sb("to_slot", [P, SHORT, WINDOW, P], fp16)
        to_node = sb("to_node", [P, SHORT, WINDOW, P], fp16)
        slots = sb("slots", [P, LONG, 9], fp32)
        row_f = sb("row_f", [P, LONG, 1], fp32)
        row_id = sb("row_id", [P, LONG, 1], i32)
        slot_node = sb("slot_node", [P, LONG, P], fp16)
        scrap = sb("scrap_f", [P, SHORT, P], fp32)
        count = sb("count", [P, LONG, 2], fp32)
        inverse = sb("inverse", [P, LONG, 2], fp32)
        factor = sb("factor", [P, LONG, 2], fp32)
        has_edge = sb("has_edge", [P, LONG, P], bf16)
        stats = sb("stats", [P, SHORT, 2, 6], fp32)
        moments = sb("moments", [P, LONG, 2, 2], fp32)
        shifted = sb("shifted", [P, LONG, 2], fp32)
        norm = sb("norm", [P, LONG, 2, 2], fp32)
        norm_in = sb("norm_in", [P, LONG, 2, 2], fp32)
        power = sb("power", [P, 2], fp32)
        eps = sb("eps", [P, 2], fp32)
        own_h = sb("own_h", [P, SHORT, D], fp32)
        self_hi = sb("self_hi", [P, SHORT, D], fp16)
        self_lo = sb("self_lo", [P, SHORT, D], fp16)
        far_hi = sb("far_hi", [P, SHORT, D], fp16)
        far_lo = sb("far_lo", [P, SHORT, D], fp16)
        turned = sb("turned", [P, SHORT, 2, 2, FC, P], fp16)

        h_bank, mean_bank, self_bank, far_bank, slot_bank, place_bank = banks[0:6]
        out_banks = banks[6:8]

        own_in = [sem(f"own_in{i}") for i in range(LONG)]
        far_in = [sem(f"far_in{i}") for i in range(LONG)]
        stored = [sem(f"stored{i}") for i in range(MID)]
        power_set, slots_set = sem("power_set"), sem("slots_set")
        windowed = sem("windowed")
        local_done, begun_done, cargo_done, sent_done = sem("local_done"), sem("begun_done"), sem("cargo_done"), sem("sent_done")
        place_done, onehots_done = sem("place_done"), sem("onehots_done")
        slots_done, row_f_done, rows_known, slot_node_done = sem("slots_done"), sem("row_f_done"), sem("rows_known"), sem("slot_node_done")
        degree_done, count_done, inverse_done, factor_done = (
            sem("degree_done"), sem("count_done"), sem("inverse_done"), sem("factor_done"))
        stats_done, moments_done = sem("stats_done"), sem("moments_done")
        shift_done, norm_in_done = sem("shift_done"), sem("norm_in_done")
        h_lo_done, mean_lo_done, self_lo_done, far_lo_done, result_done = (
            sem("h_lo_done"), sem("mean_lo_done"), sem("self_lo_done"), sem("far_lo_done"), sem("result_done"))
        shifted_done, rstd_done = sem("shifted_done"), sem("rstd_done")
        h_hi_done, mean_hi_done, self_f_done, self_hi_done, far_f_done, far_hi_done, own_h_done = (
            sem("h_hi_done"), sem("mean_hi_done"), sem("self_f_done"), sem("self_hi_done"), sem("far_f_done"),
            sem("far_hi_done"), sem("own_h_done"))
        place_ready, slots_ready, h_turned, mean_ready, out_ready = (
            sem("place_ready"), sem("slots_ready"), sem("h_turned"), sem("mean_ready"), sem("out_ready"))

        AHEAD = 8
        LOOP_FROM = 4
        TURNS = max(0, (TILES - AHEAD - LOOP_FROM) // UNROLL)

        def run(engine, step):
            def at(turn, c):
                def tile(k):
                    t = Tile(turn, c + k)
                    return t if t.exists(TILES) else None
                return tile
            for c in range(-AHEAD, LOOP_FROM):
                step(at(0, c))
            if TURNS:
                with engine.Fori(0, TURNS) as turn:
                    for c in range(LOOP_FROM, LOOP_FROM + UNROLL):
                        step(at(turn, c))
            for c in range(LOOP_FROM + TURNS * UNROLL, TILES + 1):
                step(at(0, c))

        def is_last(t):
            return t.static and t.index == TILES - 1

        with nc.Block(name="fast") as block:
            @block.sync
            def _(sp):
                def step(at):
                    if t := at(-1):
                        after(sp, result_done, t)
                        if is_last(t):
                            sp.dma_start(out[s.N - s.LAST_NEW:s.N, :], result[P - s.LAST_NEW:P, t.slot(MID), :])\
                                .then_inc(stored[t.slot(MID)], 16)
                        else:
                            sp.dma_start(out[bass.ds(t.index * P, P), :], result[:, t.slot(MID), :])\
                                .then_inc(stored[t.slot(MID)], 16)
                    if t := at(5):
                        after(sp, result_done, t, LONG)
                        first = s.LAST_BASE if is_last(t) else t.index * P
                        sp.dma_start(own[:, t.slot(LONG), :], x[bass.ds(first, P), :])\
                            .then_inc(own_in[t.slot(LONG)], 16)

                run(sp, step)
                for n in range(max(0, TILES - MID), TILES):
                    t = Tile(0, n)
                    sp.wait_ge(stored[t.slot(MID)], 16 * t.nth(MID))

            @block.gpsimd
            def _(pool):
                pool.memset(power[:, :], -0.5).then_inc(power_set, 1)
                pool.memset(eps[:, :], EPS).then_inc(power_set, 1)
                pool.memset(far[:, :, :], 0.0).then_inc(power_set, 1)
                pool.wait_ge(power_set, 3)

                last_row = pool.alloc_register("last_row")
                pool.reg_mov(last_row, s.N - 1)

                def step(at):
                    if t := at(8):
                        after(pool, cargo_done, t, LONG)
                        after(pool, sent_done, t, LONG)
                        first = pool.value_load(tinfo[0:1, 0, bass.ds(t.index, 1)], min_val=0, max_val=s.COLS)
                        pool.tensor_copy(window[:, t.slot(LONG), :, :], table[:, bass.ds(first, WINDOW), :])\
                            .then_inc(windowed, 1)
                    g, n = at(5), at(3)
                    if g:
                        after(pool, rows_known, g)
                        after(pool, far_hi_done, g, LONG)
                    if n:
                        b = n.slot(LONG)
                        after(pool, moments_done, n)
                        pool.tensor_tensor(shifted[:, b, :], moments[:, b, :, 1], eps[:, :], ALU.add)\
                            .then_inc(shifted_done, 1)
                    if g:
                        pool.indirect_dma_start(
                            out=far[:, g.slot(LONG), :], out_offset=None, in_=x[:, :],
                            in_offset=bass.IndirectOffsetOnAxis(ap=row_id[:, g.slot(LONG), :], axis=0),
                            bounds_check=last_row, oob_is_err=False).then_inc(far_in[g.slot(LONG)], 16)
                    if n:
                        after(pool, shifted_done, n)
                        pool.tensor_tensor(norm[:, b, 0, :], shifted[:, b, :], power[:, :], ALU.pow)\
                            .then_inc(rstd_done, 1)

                run(pool, step)

            @block.scalar
            def _(act):
                def step(at):
                    if t := at(1):
                        after(act, h_turned, t)
                        after(act, out_ready, t, SHORT)
                        act.activation(turned[:, t.slot(SHORT), 0, 0], h_bank[:, :], ACT.Copy, scale=SCALE)\
                            .then_inc(h_hi_done, 1)
                        after(act, mean_ready, t)
                        act.activation(turned[:, t.slot(SHORT), 1, 0], mean_bank[:, :], ACT.Copy)\
                            .then_inc(mean_hi_done, 1)
                    if t := at(2):
                        b, d = t.slot(LONG), t.slot(SHORT)
                        after(act, norm_in_done, t)
                        after(act, self_lo_done, t, 1)
                        act.activation(self_bank[:, :], own[:, b, :], ACT.Relu, bias=norm_in[:, b, 1, 0:1],
                                       scale=norm_in[:, b, 0, 0:1]).then_inc(self_f_done, 1)
                        after(act, mean_ready, t, SHORT)
                        act.activation(self_hi[:, d, :], own[:, b, :], ACT.Relu, bias=norm_in[:, b, 1, 0:1],
                                       scale=norm_in[:, b, 0, 0:1]).then_inc(self_hi_done, 1)
                        after(act, far_lo_done, t, 1)
                        act.activation(far_bank[:, :], far[:, b, :], ACT.Relu, bias=norm_in[:, b, 1, 1:2],
                                       scale=norm_in[:, b, 0, 1:2]).then_inc(far_f_done, 1)
                        act.activation(far_hi[:, d, :], far[:, b, :], ACT.Relu, bias=norm_in[:, b, 1, 1:2],
                                       scale=norm_in[:, b, 0, 1:2]).then_inc(far_hi_done, 1)
                        after(act, h_turned, t, SHORT)
                        act.activation(own_h[:, d, :], own[:, b, :], ACT.Relu, bias=norm[:, b, 1, 0:1],
                                       scale=norm[:, b, 0, 0:1]).then_inc(own_h_done, 1)

                run(act, step)

            @block.vector
            def _(dve):
                dve.memset(slots[:, :, 8], 1.0).then_inc(slots_set, 1)
                dve.wait_ge(slots_set, 1)

                def step(at):
                    if t := at(2):
                        b = t.slot(LONG)
                        after(dve, rstd_done, t)
                        dve.scalar_tensor_tensor(norm[:, b, 1, :], moments[:, b, :, 0], -1.0, norm[:, b, 0, :],
                                                 ALU.mult, ALU.mult).then_inc(shift_done, 1)
                        after(dve, shift_done, t)
                        dve.tensor_tensor(norm_in[:, b, :, :], norm[:, b, :, :],
                                          factor[:, b:b + 1, :].broadcast_to([P, 2, 2]), ALU.mult)\
                            .then_inc(norm_in_done, 1)
                    if t := at(1):
                        d = t.slot(SHORT)
                        after(dve, h_hi_done, t)
                        dve.scalar_tensor_tensor(turned[:, d, 0, 1], h_bank[:, :], SCALE, turned[:, d, 0, 0],
                                                 ALU.mult, ALU.subtract).then_inc(h_lo_done, 1)
                        after(dve, mean_hi_done, t)
                        dve.tensor_tensor(turned[:, d, 1, 1], mean_bank[:, :], turned[:, d, 1, 0],
                                          ALU.subtract).then_inc(mean_lo_done, 1)
                    if t := at(-1):
                        after(dve, out_ready, t)
                        if not t.static or t.index >= MID:
                            dve.wait_ge(stored[t.slot(MID)], 16 * (t.nth(MID) - 1))
                        dve.scalar_tensor_tensor(result[:, t.slot(MID), :], out_banks[t.slot(2)][:, :], fold[:, :],
                                                 own[:, t.slot(LONG), :], ALU.mult, ALU.add)\
                            .then_inc(result_done, 1)
                    if t := at(5):
                        b = t.slot(LONG)
                        after(dve, slots_ready, t)
                        dve.tensor_copy(slots[:, b, 0:7], slot_bank[:, 0:7]).then_inc(slots_done, 1)
                        dve.tensor_scalar(has_edge[:, b, :], slot_bank[:, P:2 * P], 1.0, None, ALU.min)
                        after(dve, slots_done, t)
                        dve.scalar_tensor_tensor(row_f[:, b, :], slots[:, b, 0:1], 256.0, slots[:, b, 1:2],
                                                 ALU.mult, ALU.add).then_inc(row_f_done, 1)
                        dve.tensor_scalar(slot_node[:, b, :], from1[:, :], slots[:, b, 4:5], None, ALU.is_equal)\
                            .then_inc(slot_node_done, 1)
                        after(dve, row_f_done, t)
                        dve.tensor_scalar(row_id[:, b, :], row_f[:, b, :], FAR, None, ALU.add).then_inc(rows_known, 1)
                        after(dve, slot_node_done, t)
                        dve.tensor_tensor_reduce(out=scrap[:, t.slot(SHORT), :], in0=slot_bank[:, P:2 * P],
                                                 in1=slot_node[:, b, :], scale=1.0, scalar=0.0, op0=ALU.mult,
                                                 op1=ALU.add, accum_out=slots[:, b, 7:8]).then_inc(degree_done, 1)
                        after(dve, degree_done, t)
                        dve.tensor_scalar(count[:, b, :], slots[:, b, 5:8:2], 1.0, None, ALU.max)\
                            .then_inc(count_done, 1)
                        after(dve, count_done, t)
                        dve.reciprocal(inverse[:, b, :], count[:, b, :]).then_inc(inverse_done, 1)
                    if t := at(3):
                        b, d = t.slot(LONG), t.slot(SHORT)
                        dve.wait_ge(own_in[b], 16 * t.nth(LONG))
                        dve.bn_stats(stats[:, d, 0, :], own[:, b, :])
                        dve.wait_ge(far_in[b], 16 * t.nth(LONG))
                        dve.bn_stats(stats[:, d, 1, :], far[:, b, :]).then_inc(stats_done, 1)
                    if t := at(5):
                        b = t.slot(LONG)
                        if u := at(3):
                            after(dve, stats_done, u)
                        after(dve, inverse_done, t)
                        dve.scalar_tensor_tensor(factor[:, b, :], inverse[:, b, :], SCALE, slots[:, b, 6:9:2],
                                                 ALU.mult, ALU.mult).then_inc(factor_done, 1)
                    if t := at(3):
                        b, d = t.slot(LONG), t.slot(SHORT)
                        if t.static:
                            after(dve, stats_done, t)
                        dve.bn_aggr(moments[:, b, 0, :], stats[:, d, 0, :])
                        dve.bn_aggr(moments[:, b, 1, :], stats[:, d, 1, :]).then_inc(moments_done, 1)
                    if t := at(2):
                        d = t.slot(SHORT)
                        after(dve, self_hi_done, t)
                        after(dve, mean_ready, t, SHORT)
                        dve.tensor_tensor(self_lo[:, d, :], self_bank[:, :], self_hi[:, d, :], ALU.subtract)\
                            .then_inc(self_lo_done, 1)
                        after(dve, far_hi_done, t)
                        dve.tensor_tensor(far_lo[:, d, :], far_bank[:, :], far_hi[:, d, :], ALU.subtract)\
                            .then_inc(far_lo_done, 1)
                    if t := at(6):
                        b, d = t.slot(LONG), t.slot(SHORT)
                        after(dve, place_ready, t)
                        dve.scalar_tensor_tensor(place[:, b, :], place_bank[:, 0:WINDOW], 1.0, sent[:, b, :],
                                                 ALU.add, ALU.mult).then_inc(place_done, 1)
                        after(dve, slots_ready, t, SHORT)
                        for j in range(WINDOW):
                            dve.tensor_scalar(to_node[:, d, j, :], from0[:, :], local[:, b, j:j + 1], None,
                                              ALU.is_equal)
                        after(dve, place_done, t)
                        for j in range(WINDOW):
                            last = dve.tensor_scalar(to_slot[:, d, j, :], from1[:, :], place[:, b, j:j + 1], None,
                                                     ALU.is_equal)
                        last.then_inc(onehots_done, 1)
                    if t := at(7):
                        b = t.slot(LONG)
                        after(dve, windowed, t)
                        dve.tensor_scalar(local[:, b, :], window[:, b, :, 0], base_of[:, bass.ds(t.index, 1)], None,
                                          ALU.subtract).then_inc(local_done, 1)
                        dve.tensor_copy(cargo[:, b, :, 0:4], window[:, b, :, 2:6])
                        after(dve, local_done, t)
                        dve.scalar_tensor_tensor(begun[:, b, :], local[:, b, :], 0.0, window[:, b, :, 1],
                                                 ALU.is_ge, ALU.mult).then_inc(begun_done, 1)
                        dve.tensor_scalar(cargo[:, b, :, 4], local[:, b, :], 1.0, 200.0, ALU.add, ALU.min)\
                            .then_inc(cargo_done, 1)
                        after(dve, begun_done, t)
                        dve.scalar_tensor_tensor(sent[:, b, :], local[:, b, :], float(P), begun[:, b, :],
                                                 ALU.is_lt, ALU.mult).then_inc(sent_done, 1)

                run(dve, step)

            @block.tensor
            def _(pe):
                def step(at):
                    if t := at(1):
                        b, d = t.slot(LONG), t.slot(SHORT)
                        after(pe, own_h_done, t)
                        after(pe, h_lo_done, t, 1)
                        for f in range(FC):
                            last = pe.transpose(h_bank[:, f * P:(f + 1) * P], own_h[:, d, f * P:(f + 1) * P],
                                                ident[:, :])
                        last.then_inc(h_turned, 1)
                        after(pe, self_lo_done, t)
                        after(pe, far_lo_done, t)
                        after(pe, mean_lo_done, t, 1)
                        for f in range(FC):
                            c = slice(f * P, (f + 1) * P)
                            terms = ((self_hi, ident16[:, :]), (self_lo, ident16[:, :]),
                                     (far_hi, slot_node[:, b, :]), (far_lo, slot_node[:, b, :]))
                            for n, (part, nodes) in enumerate(terms):
                                last = pe.matmul(mean_bank[:, c], part[:, d, c], nodes,
                                                 start=(n == 0), stop=(n == len(terms) - 1))
                        last.then_inc(mean_ready, 1)
                    if t := at(5):
                        b, d = t.slot(LONG), t.slot(SHORT)
                        after(pe, onehots_done, t)
                        after(pe, degree_done, t, 1)
                        for j in range(WINDOW):
                            pe.matmul(slot_bank[:, 0:5], to_slot[:, d, j, :], cargo[:, b, j, :],
                                      start=(j == 0), stop=(j == WINDOW - 1))
                        for j in range(WINDOW):
                            pe.matmul(slot_bank[:, 5:7], to_node[:, d, j, :], cargo[:, b, j, 2:4],
                                      start=(j == 0), stop=(j == WINDOW - 1))
                        for j in range(WINDOW):
                            last = pe.matmul(slot_bank[:, P:2 * P], ones16[:, :], to_node[:, d, j, :],
                                             start=(j == 0), stop=(j == WINDOW - 1))
                        last.then_inc(slots_ready, 1)
                    if t := at(6):
                        b = t.slot(LONG)
                        after(pe, sent_done, t)
                        after(pe, place_done, t, 1)
                        pe.matmul(place_bank[:, 0:WINDOW], upper[:, :], sent[:, b, :], start=True, stop=False)
                        for j in range(1, WINDOW):
                            last = pe.matmul(place_bank[:, j:WINDOW], ones16[:, :], sent[:, b, 0:WINDOW - j],
                                             start=False, stop=(j == WINDOW - 1))
                        last.then_inc(place_ready, 1)
                    if t := at(0):
                        b, d = t.slot(LONG), t.slot(SHORT)
                        after(pe, mean_lo_done, t)
                        after(pe, result_done, t, 2)
                        bank = out_banks[t.slot(2)]
                        pe.matmul(bank[:, :], has_edge[:, b, :], bias3[:, :], start=True, stop=False)
                        for k in range(2):
                            for f in range(FC):
                                for hi_lo, part in ((0, 0), (0, 1), (1, 0)):
                                    last = pe.matmul(bank[:, :], turned[:, d, k, hi_lo, f, :],
                                                     weights[:, k, part, f, :], start=False,
                                                     stop=(k == 1 and f == FC - 1 and hi_lo == 1))
                        last.then_inc(out_ready, 1)

                run(pe, step)


def general(nc, s):
    x, out, D, FC, TILES = s.x, s.out, s.D, s.FC, s.TILES
    ident, ones16, from0 = s.ident, s.ones16, s.from0
    weights, bias3, fold, table, tinfo, banks = s.weights, s.bias3, s.fold, s.table, s.tinfo, s.banks
    with ExitStack() as ctx:
        def sb(name, shape, dt):
            return ctx.enter_context(nc.sbuf_tensor(name, shape, dt))

        def sem(name):
            return ctx.enter_context(nc.semaphore(name))

        own = sb("g_own", [P, D], fp32)
        far = sb("g_far", [P, D], fp32)
        result = sb("g_result", [P, D], fp32)
        row_id = sb("g_row_id", [P, 1], i32)
        base = sb("g_base", [P, 1], fp32)
        local = sb("g_local", [P, 1], fp32)
        to_node = sb("g_to_node", [P, P], fp16)
        zeros = sb("g_zeros", [P, D], fp16)
        stats = sb("g_stats", [P, 6], fp32)
        moments = sb("g_moments", [P, 2], fp32)
        shifted = sb("g_shifted", [P, 1], fp32)
        power = sb("g_power", [P, 1], fp32)
        eps = sb("g_eps", [P, 1], fp32)
        rstd = sb("g_rstd", [P, 1], fp32)
        shift = sb("g_shift", [P, 1], fp32)
        h = sb("g_h", [P, D], fp32)
        h_hi = sb("g_h_hi", [P, D], fp16)
        h_lo = sb("g_h_lo", [P, D], fp16)
        inverse = sb("g_inverse", [P, P], fp32)
        mean = sb("g_mean", [P, FC, P], fp32)
        has_edge = sb("g_has_edge", [P, P], bf16)
        turned = sb("g_turned", [P, 2, 2, FC, P], fp16)
        h_bank, mean_bank, degree_bank, out_bank = banks[0:4]

        own_in, far_in, stored = sem("g_own_in"), sem("g_far_in"), sem("g_stored")
        pool_own, dve_own = sem("g_pool_own"), sem("g_dve_own")
        set_up = sem("g_set_up")
        moments_done, rstd_done, item_ready, item_used = (
            sem("g_moments"), sem("g_rstd"), sem("g_item_ready"), sem("g_item_used"))
        mean_split, out_ready, result_done = sem("g_mean_split"), sem("g_out_ready"), sem("g_result_done")

        class Count:

            def __init__(self, engine, name):
                self.engine, self.reg = engine, engine.alloc_register(name)
                engine.reg_mov(self.reg, 0)

            def value(self):
                return self.engine.snap(self.reg)

            def add(self):
                self.engine.reg_add(self.reg, self.reg, 1)

        def flagged(engine, own_part, chunk_part, tile_part):
            with engine.If(engine.value_load(s.n_general[0:1, 0:1], min_val=0, max_val=TILES) > 0):
                with engine.Fori(0, TILES) as t:
                    flag = engine.value_load(tinfo[0:1, 2, bass.ds(t, 1)], min_val=0, max_val=1)
                    with engine.If(flag > 0):
                        own_part(t)
                        first = engine.value_load(tinfo[0:1, 0, bass.ds(t, 1)], min_val=0, max_val=s.COLS)
                        end = engine.value_load(tinfo[0:1, 1, bass.ds(t, 1)], min_val=0, max_val=s.COLS)
                        with engine.Fori(first, end) as chunk:
                            chunk_part(engine.snap(chunk, min_val=0, max_val=s.COLS - 1))
                        tile_part(t)

        with nc.Block(name="general") as block:
            @block.gpsimd
            def _(pool):
                items, tiles, chunks, own_steps = (Count(pool, "pool_items"), Count(pool, "pool_tiles"),
                                                   Count(pool, "pool_chunks"), Count(pool, "pool_steps"))
                pool.memset(power[:, :], -0.5).then_inc(set_up, 1)
                pool.memset(eps[:, :], EPS).then_inc(set_up, 1)
                pool.memset(zeros[:, :], 0.0).then_inc(set_up, 1)
                pool.wait_ge(set_up, 3)

                last_row = pool.alloc_register("g_last_row")
                pool.reg_mov(last_row, s.N - 1)

                def own_step(ins):
                    ins.then_inc(pool_own, 1)
                    pool.wait_ge(pool_own, own_steps.value() + 1)
                    own_steps.add()

                def normalise():
                    pool.wait_ge(moments_done, items.value() + 1)
                    own_step(pool.tensor_tensor(shifted[:, :], moments[:, 1:2], eps[:, :], ALU.add))
                    pool.tensor_tensor(rstd[:, :], shifted[:, :], power[:, :], ALU.pow).then_inc(rstd_done, 1)
                    pool.wait_ge(item_used, items.value() + 1)
                    items.add()

                def own_part(t):
                    first = pool.value_load(tinfo[0:1, 3, bass.ds(t, 1)], min_val=0, max_val=s.LAST_BASE)
                    pool.dma_start(own[:, :], x[bass.ds(first, P), :]).then_inc(own_in, 16)
                    normalise()

                def chunk_part(chunk):
                    own_step(pool.tensor_copy(row_id[:, :], s.src_of[:, bass.ds(chunk, 1)]))
                    pool.indirect_dma_start(
                        out=far[:, :], out_offset=None, in_=x[:, :],
                        in_offset=bass.IndirectOffsetOnAxis(ap=row_id[:, :], axis=0),
                        bounds_check=last_row, oob_is_err=False).then_inc(far_in, 16)
                    normalise()

                def tile_part(t):
                    pool.wait_ge(result_done, tiles.value() + 1)
                    tiles.add()
                    first = pool.value_load(tinfo[0:1, 3, bass.ds(t, 1)], min_val=0, max_val=s.LAST_BASE)
                    pool.dma_start(out[bass.ds(first, P), :], result[:, :]).then_inc(stored, 16)
                    pool.wait_ge(stored, tiles.value() * 16)

                flagged(pool, own_part, chunk_part, tile_part)

            @block.vector
            def _(dve):
                items, tiles, chunks, own_steps = (Count(dve, "dve_items"), Count(dve, "dve_tiles"),
                                                   Count(dve, "dve_chunks"), Count(dve, "dve_steps"))

                def own_step(ins):
                    ins.then_inc(dve_own, 1)
                    own_steps.add()
                    dve.wait_ge(dve_own, own_steps.value())

                def normalise(rows, meanwhile):
                    own_step(dve.bn_stats(stats[:, :], rows))
                    meanwhile()
                    dve.bn_aggr(moments[:, :], stats[:, :]).then_inc(moments_done, 1)
                    dve.wait_ge(rstd_done, items.value() + 1)
                    own_step(dve.scalar_tensor_tensor(shift[:, :], moments[:, 0:1], -1.0, rstd[:, :],
                                                      ALU.mult, ALU.mult))
                    own_step(dve.tensor_scalar(h[:, :], rows, rstd[:, :], shift[:, :], ALU.mult, ALU.add))

                def own_part(t):
                    dve.wait_ge(own_in, tiles.value() * 16 + 16)
                    normalise(own[:, :], lambda: dve.tensor_copy(base[:, :], tinfo[:, 3, bass.ds(t, 1)]))
                    dve.tensor_scalar(h[:, :], h[:, :], 0.0, None, ALU.max).then_inc(item_ready, 1)
                    dve.wait_ge(item_used, items.value() + 1)
                    own_step(dve.tensor_scalar(turned[:, 0, 0], h_bank[:, :], SCALE, None, ALU.mult))
                    own_step(dve.scalar_tensor_tensor(turned[:, 0, 1], h_bank[:, :], SCALE, turned[:, 0, 0],
                                                      ALU.mult, ALU.subtract))
                    items.add()

                def chunk_part(chunk):
                    dve.wait_ge(far_in, chunks.value() * 16 + 16)

                    def nodes():
                        own_step(dve.tensor_scalar(local[:, :], table[:, bass.ds(chunk, 1), 0], base[:, :], None,
                                                   ALU.subtract))
                        dve.tensor_scalar(to_node[:, :], from0[:, :], local[:, :], None, ALU.is_equal)

                    normalise(far[:, :], nodes)
                    own_step(dve.tensor_scalar(h[:, :], h[:, :], 0.0, SCALE, ALU.max, ALU.mult))
                    own_step(dve.tensor_copy(h_hi[:, :], h[:, :]))
                    dve.tensor_tensor(h_lo[:, :], h[:, :], h_hi[:, :], ALU.subtract).then_inc(item_ready, 1)
                    dve.wait_ge(item_used, items.value() + 1)
                    items.add()
                    chunks.add()

                def tile_part(t):
                    own_step(dve.tensor_scalar(inverse[:, :], degree_bank[:, 0:P], 1.0, None, ALU.max))
                    own_step(dve.reciprocal(inverse[:, :], inverse[:, :]))
                    dve.tensor_scalar(has_edge[:, :], degree_bank[:, 0:P], 1.0, None, ALU.min)
                    for f in range(FC):
                        last = dve.tensor_tensor(mean[:, f, :], mean_bank[:, f * P:(f + 1) * P], inverse[:, :], ALU.mult)
                    own_step(last)
                    own_step(dve.tensor_copy(turned[:, 1, 0], mean[:, :, :]))
                    dve.tensor_tensor(turned[:, 1, 1], mean[:, :, :], turned[:, 1, 0], ALU.subtract)\
                        .then_inc(mean_split, 1)
                    dve.wait_ge(out_ready, tiles.value() + 1)
                    dve.scalar_tensor_tensor(result[:, :], out_bank[:, :], fold[:, :], own[:, :],
                                             ALU.mult, ALU.add).then_inc(result_done, 1)
                    tiles.add()

                dve.wait_ge(set_up, 3)
                flagged(dve, own_part, chunk_part, tile_part)

            @block.tensor
            def _(pe):
                items, tiles = Count(pe, "pe_items"), Count(pe, "pe_tiles")
                pe.wait_ge(set_up, 3)

                def own_part(t):
                    pe.wait_ge(item_ready, items.value() + 1)
                    for f in range(FC):
                        last = pe.transpose(h_bank[:, f * P:(f + 1) * P], h[:, f * P:(f + 1) * P], ident[:, :])
                    pe.matmul(mean_bank[:, :], zeros[:, 0:P], zeros[:, :], start=True, stop=False,
                              skip_group_check=True)
                    last = pe.matmul(degree_bank[:, 0:P], zeros[:, 0:P], zeros[:, 0:P], start=True, stop=False,
                                     skip_group_check=True)
                    last.then_inc(item_used, 1)
                    items.add()

                def chunk_part(chunk):
                    pe.wait_ge(item_ready, items.value() + 1)
                    for f in range(FC):
                        c = slice(f * P, (f + 1) * P)
                        for part in (h_hi, h_lo):
                            pe.matmul(mean_bank[:, c], part[:, c], to_node[:, :], start=False, stop=False,
                                      skip_group_check=True)
                    pe.matmul(degree_bank[:, 0:P], ones16[:, :], to_node[:, :], start=False, stop=False,
                              skip_group_check=True).then_inc(item_used, 1)
                    items.add()

                def tile_part(t):
                    pe.wait_ge(mean_split, tiles.value() + 1)
                    pe.matmul(out_bank[:, :], has_edge[:, :], bias3[:, :], start=True, stop=False)
                    for k in range(2):
                        for f in range(FC):
                            for hi_lo, part in ((0, 0), (0, 1), (1, 0)):
                                last = pe.matmul(out_bank[:, :], turned[:, k, hi_lo, f, :], weights[:, k, part, f, :],
                                                 start=False, stop=(k == 1 and f == FC - 1 and hi_lo == 1))
                    last.then_inc(out_ready, 1)
                    tiles.add()

                flagged(pe, own_part, chunk_part, tile_part)


_INS = ["x", "src", "dst", "L0_gnn_W_l", "L0_gnn_b_l", "L0_gnn_W_r"]


def kernel(**inputs):
    import numpy as _np
    import concourse.bacc as _bacc
    from concourse import mybir as _mybir
    from concourse.bass_utils import run_bass_kernel_spmd as _run

    nc = _bacc.Bacc("TRN2", target_bir_lowering=False, num_devices=1)
    arrays, args = {}, []
    for name in _INS:
        a = _np.ascontiguousarray(inputs[name])
        arrays[f"in_{name}_dram"] = a
        args.append(nc.dram_tensor(f"in_{name}_dram", a.shape, _mybir.dt.from_np(a.dtype), kind="ExternalInput").ap())
    shape = arrays["in_x_dram"].shape
    out = nc.dram_tensor("out_0_dram", shape, _mybir.dt.float32, kind="ExternalOutput").ap()
    gnn_kernel(nc, *args, out)
    r = _run(nc, [arrays], core_ids=[0])
    return r.results[0]["out_0_dram"]
```

```python
from contextlib import ExitStack

import concourse.bass as bass
from concourse import mybir

P = 128
HALO = 16
SUB = 64
UNROLL = 6
LOOP_FROM = 4
DENSE_AHEAD = 5
UNITS_AHEAD = 8
LONG, MID, SHORT = 6, 3, 2
FAR = float(1 << 17)
SCALE = 256.0
EPS = 1e-5

fp32, fp16, i32 = mybir.dt.float32, mybir.dt.float16, mybir.dt.int32
ALU = mybir.AluOpType
ACT = mybir.ActivationFunctionType
AX = mybir.AxisListType
RMAX = bass.bass_isa.ReduceOp.max


class Shared:
    pass


class Tile:

    def __init__(self, turn, c):
        self.turn, self.c = turn, c
        self.index = turn * UNROLL + c
        self.static = isinstance(turn, int)

    def slot(self, depth):
        return self.c % depth

    def nth(self, depth):
        return self.turn * (UNROLL // depth) + self.c // depth + 1


def after(engine, semaphore, tile, lag=0, by=1):
    value = tile.index - lag + 1
    if tile.static and value <= 0:
        return
    engine.wait_ge(semaphore, value * by)


def gnn_kernel(nc, x, src, dst, w_l, b_l, w_r, out):
    N, D = x.shape
    E = src.shape[0]
    FC = D // P
    TILES = -(-N // P)
    LAST_BASE = N - P
    LAST_NEW = N - (TILES - 1) * P
    CHUNKS = -(-E // P)
    EG = -(-CHUNKS // P)
    COLS = EG * P
    NSUB = P // SUB
    ROW = EG * NSUB * P
    TG = -(-TILES // P)
    TCOLS = TG * P
    W = -(-E // P)
    DENSE_TURNS = (TILES - DENSE_AHEAD - LOOP_FROM) // UNROLL
    SENDS = -(-W // (2 * (DENSE_TURNS + 1)))
    RCOLS = SENDS * 2 * (DENSE_TURNS + 1)
    MAX_TURNS = -(-E // (UNROLL * P))
    UNITS = MAX_TURNS * UNROLL + LOOP_FROM + UNITS_AHEAD + 1
    assert W <= 2048 and MAX_TURNS <= P and UNITS * P <= FAR and N <= FAR and HALO <= W

    ctx = ExitStack()
    with ctx:
        def sb(name, shape, dt):
            return ctx.enter_context(nc.sbuf_tensor(name, shape, dt))

        ident = sb("ident", [P, P], fp32)
        ones = sb("ones", [P, P], fp32)
        ones16 = sb("ones16", [P, P], fp16)
        upper = sb("upper", [P, P], fp16)
        lower = sb("lower", [P, P], fp16)
        from0 = sb("from0", [P, P], fp32)
        weights = sb("weights", [P, 2, 2, FC, D], fp16)
        bias = sb("bias", [P, D], fp32)
        fold = sb("fold", [P, 1], fp32)
        record = sb("record", [P, RCOLS, 4], i32)
        goes_to = sb("goes_to", [P, RCOLS], i32)
        turns = sb("turns", [P, 1], i32)
        n_bad = sb("n_bad", [P, 1], i32)
        records = nc.dram_tensor("records", [UNITS * P, 4], i32, kind="Internal").ap()

        banks = [ctx.enter_context(nc.psum_tensor(f"bank{i}", [P, 512], fp32)) for i in range(8)]

        s = Shared()
        s.x, s.src, s.dst, s.w_l, s.b_l, s.w_r, s.out = x, src, dst, w_l, b_l, w_r, out
        (s.N, s.D, s.E, s.FC, s.TILES, s.LAST_BASE, s.LAST_NEW, s.EG, s.COLS, s.NSUB, s.ROW, s.TG, s.TCOLS) = (
            N, D, E, FC, TILES, LAST_BASE, LAST_NEW, EG, COLS, NSUB, ROW, TG, TCOLS)
        s.W, s.DENSE_TURNS, s.SENDS, s.RCOLS, s.MAX_TURNS, s.UNITS = W, DENSE_TURNS, SENDS, RCOLS, MAX_TURNS, UNITS
        (s.ident, s.ones, s.ones16, s.upper, s.lower, s.from0) = (ident, ones, ones16, upper, lower, from0)
        (s.weights, s.bias, s.fold, s.record, s.goes_to, s.turns, s.n_bad, s.records, s.banks) = (
            weights, bias, fold, record, goes_to, turns, n_bad, records, banks)
        prepare(nc, s)
        dense(nc, s)
        correct(nc, s)
        table = sb("table", [P, COLS, 4], fp32)
        s.table = table
        s.src_of = sb("src_of", [P, COLS], i32)
        s.tinfo = sb("tinfo", [P, 3, TCOLS], i32)
        ranges(nc, s)
        general(nc, s)


def prepare(nc, s):
    D, E, N, FC, W, RCOLS = s.D, s.E, s.N, s.FC, s.W, s.RCOLS
    ident, ones, ones16, upper, lower, from0 = s.ident, s.ones, s.ones16, s.upper, s.lower, s.from0
    weights, bias, fold, record, goes_to, banks = s.weights, s.bias, s.fold, s.record, s.goes_to, s.banks
    L = W + 2 * HALO
    HERE = slice(HALO, HALO + W)
    STEPS = (W - 1).bit_length()
    PAD = 1 << (STEPS - 1)
    with ExitStack() as ctx:
        def sb(name, shape, dt):
            return ctx.enter_context(nc.sbuf_tensor(name, shape, dt))

        def sem(name):
            return ctx.enter_context(nc.semaphore(name))

        raw_w = sb("raw_w", [P, 2, FC, D], fp32)
        raw_dst = sb("raw_dst", [P, L], i32)
        raw_src = sb("raw_src", [P, W], i32)
        node = sb("node", [P, L], fp32)
        other = sb("other", [P, W], fp32)
        differs = sb("differs", [P, L], fp32)
        position = sb("position", [P, L], fp32)
        from_end = sb("from_end", [P, L], fp32)
        left = sb("left", [P, 2, L], fp32)
        right = sb("right", [P, 2, L], fp32)
        degree = sb("degree", [P, W], fp32)
        real = sb("real", [P, W], fp32)
        crowded = sb("crowded", [P, W], fp32)
        sent = sb("sent", [P, W], fp32)
        prefix = sb("prefix", [P, 2, PAD + W], fp32)
        skip = sb("skip", [P, W], fp32)
        scrap = sb("scrap", [P, W], fp32)
        counts = sb("counts", [P, 4], fp32)
        counts16 = sb("counts16", [P, 4], fp16)
        totals = sb("totals", [P, 5], fp32)
        turn_starts = sb("turn_starts", [P, P], fp32)
        n_turns = sb("n_turns", [P, 1], fp32)
        bad = sb("bad", [P, 1], fp32)
        blank = sb("blank", [P, s.UNITS, 4], i32)
        wmax = sb("wmax", [P, 2], fp32)
        wint = sb("wint", [P, 2], i32)
        wscale = sb("wscale", [P, 1], fp32)

        w_in, b_in, e_in, blank_in = sem("w_in"), sem("b_in"), sem("e_in"), sem("blank_in")
        dst_filled, src_filled, pads_filled, blank_filled = (
            sem("dst_filled"), sem("src_filled"), sem("pads_filled"), sem("blank_filled"))
        pool_done, consts, padded = sem("pool_done"), sem("consts"), sem("padded")
        w_summed, wmax_ready, wmax_shared, wscale_ready = (
            sem("w_summed"), sem("wmax_ready"), sem("wmax_shared"), sem("wscale_ready"))
        dve_done = sem("dve_done")
        w_turned, w_hi, w_taken = sem("w_turned"), sem("w_hi"), sem("w_taken")
        counted, totalled = sem("counted"), sem("totalled")

        def edge_loads(raw, flat, halo):
            span = W + 2 * halo
            inside = [p for p in range(P) if p * W - halo >= 0 and p * W - halo + span <= E]
            lo, hi = inside[0], inside[-1] + 1
            first = lo * W - halo
            loads = [(raw[lo:hi, :], bass.AP(flat.tensor, first, [[W, hi - lo], [1, span]]))]
            for p in range(P):
                a, b = max(p * W - halo, 0), min(p * W - halo + span, E)
                if not lo <= p < hi and a < b:
                    c = a - (p * W - halo)
                    loads.append((raw[p:p + 1, c:c + b - a], flat[a:b].rearrange("(a e) -> a e", a=1)))
            return loads

        loads = edge_loads(raw_dst, s.dst, HALO) + edge_loads(raw_src, s.src, 0)

        with nc.Block(name="prepare") as block:
            @block.sync
            def _(sp):
                sp.dma_start(raw_w[:, 0, :, :], s.w_r.rearrange("(o p) f -> p o f", p=P)).then_inc(w_in, 16)
                sp.dma_start(raw_w[:, 1, :, :], s.w_l.rearrange("(o p) f -> p o f", p=P)).then_inc(w_in, 16)
                sp.dma_start(bias[:, :], s.b_l.rearrange("(a n) -> a n", a=1).broadcast_to([P, D])).then_inc(b_in, 16)
                sp.wait_ge(blank_filled, 3)
                sp.dma_start(s.records.rearrange("(p u) k -> p u k", p=P), blank[:, :, :]).then_inc(blank_in, 16)
                sp.wait_ge(b_in, 16)
                sp.wait_ge(blank_in, 16)

            @block.gpsimd
            def _(pool):
                step = [0]

                def link(ins):
                    step[0] += 1
                    ins.then_inc(pool_done, 1)
                    pool.wait_ge(pool_done, step[0])

                link(pool.memset(raw_dst[:, :], int(FAR)))
                pool.memset(raw_dst[0:1, 0:HALO], -5).then_inc(dst_filled, 1)
                pool.memset(raw_src[:, :], int(FAR)).then_inc(src_filled, 1)
                pool.iota(position[:, :], pattern=[[1, L]], base=0, channel_multiplier=0,
                          allow_small_or_imprecise_dtypes=True)
                pool.memset(ones[:, :], 1.0)
                pool.memset(ones16[:, :], 1.0)
                link(pool.memset(ident[:, :], 0.0))
                link(pool.affine_select(out=ident[:, :], in_=ident[:, :], compare_op=ALU.not_equal, fill=1.0,
                                        base=0, pattern=[[-1, P]], channel_multiplier=1))
                link(pool.memset(upper[:, :], 1.0))
                pool.affine_select(out=upper[:, :], in_=upper[:, :], compare_op=ALU.is_gt, fill=0.0,
                                   base=0, pattern=[[1, P]], channel_multiplier=-1)
                link(pool.memset(lower[:, :], 1.0))
                link(pool.affine_select(out=lower[:, :], in_=lower[:, :], compare_op=ALU.is_gt, fill=0.0,
                                        base=0, pattern=[[-1, P]], channel_multiplier=1))
                pool.iota(from0[:, :], pattern=[[1, P]], base=0, channel_multiplier=0,
                          allow_small_or_imprecise_dtypes=True).then_inc(consts, 1)
                pool.wait_ge(wmax_ready, 1)
                pool.partition_all_reduce(wmax[:, 1:2], wmax[:, 0:1], P, RMAX)\
                    .then_inc(wmax_shared, 1)
                pool.memset(prefix[:, 0, 0:PAD], 0.0).then_inc(padded, 1)
                pool.memset(prefix[:, 1, 0:PAD], 0.0).then_inc(padded, 1)
                pool.memset(record[:, :, :], 0).then_inc(pads_filled, 1)
                pool.memset(goes_to[:, :], int(FAR)).then_inc(pads_filled, 1)
                pool.memset(blank[:, :, 0:2], int(FAR)).then_inc(blank_filled, 1)
                pool.memset(blank[:, :, 2], 1).then_inc(blank_filled, 1)
                pool.memset(blank[:, :, 3], 0).then_inc(blank_filled, 1)

            @block.scalar
            def _(act):
                act.wait_ge(dst_filled, 1)
                act.wait_ge(src_filled, 1)
                for to, frm in loads:
                    act.dma_start(to, frm).then_inc(e_in, 16)
                act.wait_ge(wscale_ready, 1)
                for n in range(2 * FC):
                    k, f = divmod(n, FC)
                    act.wait_ge(w_turned, n + 1)
                    act.activation(weights[:, k, 0, f, :], banks[4 + n % 4][:, :], ACT.Copy, scale=wscale[:, :])\
                        .then_inc(w_hi, 1)

            @block.vector
            def _(dve):
                step = [0]

                def link(ins):
                    step[0] += 1
                    ins.then_inc(dve_done, 1)
                    dve.wait_ge(dve_done, step[0])

                dve.wait_ge(w_in, 32)
                ins = dve.tensor_tensor(raw_w[:, 0, :, :], raw_w[:, 0, :, :], raw_w[:, 1, :, :], ALU.add)
                ins.then_inc(w_summed, 1)
                dve.wait_ge(w_summed, 1)
                dve.tensor_reduce(wmax[:, 0:1], raw_w[:, :, :, :], AX.XYZ, ALU.max, apply_absolute_value=True)\
                    .then_inc(wmax_ready, 1)

                dve.wait_ge(e_in, 16 * len(loads))
                dve.tensor_copy(other[:, :], raw_src[:, :])
                link(dve.tensor_copy(node[:, :], raw_dst[:, :]))
                dve.tensor_tensor(differs[:, 1:L], node[:, 1:L], node[:, 0:L - 1], ALU.not_equal)
                dve.wait_ge(consts, 1)
                dve.tensor_scalar(from_end[:, :], position[:, :], -1.0, float(L), ALU.mult, ALU.add)
                dve.wait_ge(padded, 2)
                dve.tensor_tensor(sent[:, :], other[:, :], node[:, HERE], ALU.not_equal)
                dve.tensor_tensor(prefix[:, 0, PAD:PAD + W], other[:, :], node[:, HERE], ALU.not_equal)
                link(dve.tensor_tensor_reduce(out=scrap[:, :], in0=node[:, HALO - 1:HALO - 1 + W], in1=node[:, HERE],
                                              scale=1.0, scalar=0.0, op0=ALU.subtract, op1=ALU.max,
                                              accum_out=counts[:, 1:2]))
                link(dve.tensor_scalar(counts[:, 1:2], counts[:, 1:2], 1.0, None, ALU.min))

                dve.wait_ge(wmax_shared, 1)
                link(dve.tensor_scalar(wint[:, 0:1], wmax[:, 1:2].bitcast(i32), 0x7F800000, None, ALU.bitwise_and))
                link(dve.tensor_scalar(wint[:, 0:1], wint[:, 0:1], float(32 << 23), None, ALU.max))
                link(dve.tensor_scalar(wint[:, 1:2], wint[:, 0:1], -1.0, float((254 + 8) << 23), ALU.mult, ALU.add))
                dve.tensor_copy(wscale[:, :], wint[:, 1:2].bitcast(fp32)).then_inc(wscale_ready, 1)
                link(dve.tensor_scalar(wint[:, 0:1], wint[:, 0:1], float(16 << 23), None, ALU.subtract))
                dve.tensor_copy(fold[:, :], wint[:, 0:1].bitcast(fp32))

                dve.tensor_tensor(left[:, 0, 1:L], differs[:, 1:L], position[:, 1:L], ALU.mult)
                link(dve.tensor_tensor(right[:, 0, 0:L - 1], differs[:, 1:L], from_end[:, 0:L - 1], ALU.mult))
                reach = 1
                for k in range(STEPS):
                    a, b = k % 2, 1 - k % 2
                    if reach < HALO:
                        lo, hi = 2 * reach, L - 2 * reach
                        dve.tensor_tensor(left[:, b, lo:L], left[:, a, lo:L], left[:, a, lo - reach:L - reach], ALU.max)
                        dve.tensor_tensor(right[:, b, 0:hi], right[:, a, 0:hi], right[:, a, reach:hi + reach], ALU.max)
                        reach *= 2
                        spans = b
                    link(dve.tensor_tensor(prefix[:, b, PAD:], prefix[:, a, PAD:], prefix[:, a, PAD - (1 << k):PAD + W - (1 << k)],
                                           ALU.add))
                    sums = b
                    if k < 2 * FC:
                        dve.wait_ge(w_hi, k + 1)
                        wk, f = divmod(k, FC)
                        dve.scalar_tensor_tensor(weights[:, wk, 1, f, :], banks[4 + k % 4][:, :], wscale[:, :],
                                                 weights[:, wk, 0, f, :], ALU.mult, ALU.subtract).then_inc(w_taken, 1)
                for k in range(STEPS, 2 * FC):
                    dve.wait_ge(w_hi, k + 1)
                    wk, f = divmod(k, FC)
                    dve.scalar_tensor_tensor(weights[:, wk, 1, f, :], banks[4 + k % 4][:, :], wscale[:, :],
                                             weights[:, wk, 0, f, :], ALU.mult, ALU.subtract).then_inc(w_taken, 1)
                dve.tensor_scalar(real[:, :], node[:, HERE], FAR, None, ALU.is_lt)
                link(dve.tensor_tensor(degree[:, :], left[:, spans, HERE], right[:, spans, HERE], ALU.add))
                link(dve.tensor_scalar(degree[:, :], degree[:, :], -1.0, float(L + 1), ALU.mult, ALU.add))
                dve.tensor_scalar(skip[:, :], sent[:, :], -FAR, FAR, ALU.mult, ALU.add)
                link(dve.tensor_scalar(crowded[:, :], degree[:, :], float(HALO), None, ALU.is_gt))
                link(dve.tensor_tensor_reduce(out=scrap[:, :], in0=crowded[:, :], in1=real[:, :], scale=1.0, scalar=0.0,
                                              op0=ALU.mult, op1=ALU.add, accum_out=counts[:, 2:3]))
                link(dve.tensor_tensor_reduce(out=scrap[:, :], in0=differs[:, HERE], in1=real[:, :], scale=1.0,
                                              scalar=0.0, op0=ALU.mult, op1=ALU.add, accum_out=counts[:, 3:4]))
                link(dve.tensor_copy(counts[:, 0:1], prefix[:, sums, PAD + W - 1:PAD + W]))
                dve.tensor_copy(counts16[:, :], counts[:, :]).then_inc(counted, 1)

                dve.wait_ge(pads_filled, 2)
                dve.tensor_copy(record[:, 0:W, 0], raw_src[:, :])
                dve.tensor_copy(record[:, 0:W, 1], raw_dst[:, HERE])
                dve.tensor_copy(record[:, 0:W, 2], degree[:, :])
                dve.wait_ge(totalled, 1)
                link(dve.tensor_copy(totals[:, :], banks[0][:, 0:5]))
                link(dve.tensor_scalar(totals[:, 0:1], totals[:, 0:1], -1.0, None, ALU.add))
                link(dve.scalar_tensor_tensor(scrap[:, :], prefix[:, sums, PAD:PAD + W], totals[:, 0:1], sent[:, :],
                                              ALU.add, ALU.mult))
                dve.tensor_tensor(goes_to[:, 0:W], scrap[:, :], skip[:, :], ALU.add)
                link(dve.tensor_scalar(turn_starts[:, :], from0[:, :], float(UNROLL * P), float((LOOP_FROM - 2) * P),
                                       ALU.mult, ALU.add))
                link(dve.tensor_scalar(turn_starts[:, :], turn_starts[:, :], totals[:, 1:2], None, ALU.is_lt))
                link(dve.tensor_reduce(n_turns[:, :], turn_starts[:, :], AX.X, ALU.add))
                dve.tensor_scalar(s.turns[:, :], n_turns[:, :], 1.0, None, ALU.max)
                link(dve.tensor_scalar(bad[:, :], totals[:, 4:5], float(N), None, ALU.not_equal))
                link(dve.tensor_tensor(bad[:, :], bad[:, :], totals[:, 2:3], ALU.add))
                dve.tensor_tensor(s.n_bad[:, :], bad[:, :], totals[:, 3:4], ALU.add)

            @block.tensor
            def _(pe):
                pe.wait_ge(consts, 1)
                pe.wait_ge(w_summed, 1)
                for n in range(2 * FC):
                    if n >= 4:
                        pe.wait_ge(w_taken, n - 3)
                    k, f = divmod(n, FC)
                    for o in range(FC):
                        last = pe.transpose(banks[4 + n % 4][:, o * P:(o + 1) * P],
                                            raw_w[:, k, o, f * P:(f + 1) * P], ident[:, :])
                    last.then_inc(w_turned, 1)
                pe.wait_ge(counted, 1)
                pe.matmul(banks[0][:, 0:1], upper[:, :], counts16[:, 0:1], start=True, stop=True)
                pe.matmul(banks[0][:, 1:5], ones16[:, :], counts16[:, :], start=True, stop=True).then_inc(totalled, 1)


def dense(nc, s):
    x, out, D, FC, TILES = s.x, s.out, s.D, s.FC, s.TILES
    weights, bias, fold, banks, SENDS = s.weights, s.bias, s.fold, s.banks, s.SENDS
    with ExitStack() as ctx:
        def sb(name, shape, dt):
            return ctx.enter_context(nc.sbuf_tensor(name, shape, dt))

        def sem(name):
            return ctx.enter_context(nc.semaphore(name))

        own = sb("own", [P, LONG, D], fp32)
        result = sb("result", [P, MID, D], fp32)
        stats = sb("stats", [P, SHORT, 6], fp32)
        moments = sb("moments", [P, LONG, 2], fp32)
        shifted = sb("shifted", [P, LONG], fp32)
        norm = sb("norm", [P, LONG, 2], fp32)
        power = sb("power", [P, 1], fp32)
        eps = sb("eps", [P, 1], fp32)
        h = sb("h", [P, SHORT, D], fp32)
        turned = sb("turned", [P, SHORT, 2, FC, P], fp16)
        parcels = sb("parcels", [P, 2, SENDS, 4], i32)
        address = sb("address", [P, 2, SENDS], i32)

        h_banks, out_banks = banks[0:2], banks[2:4]

        own_in = [sem(f"own_in{i}") for i in range(LONG)]
        stored = [sem(f"stored{i}") for i in range(MID)]
        records_sent = [sem("records_sent0"), sem("records_sent1")]
        parcel_ready = [sem("parcel_ready0"), sem("parcel_ready1")]
        power_set = sem("power_set")
        stats_done, moments_done, shift_done, h_lo_done, base_done, result_done = (
            sem("stats_done"), sem("moments_done"), sem("shift_done"), sem("h_lo_done"), sem("base_done"),
            sem("result_done"))
        shifted_done, rstd_done = sem("shifted_done"), sem("rstd_done")
        h_done, h_hi_done = sem("h_done"), sem("h_hi_done")
        h_turned, out_ready = sem("h_turned"), sem("out_ready")

        TURNS = s.DENSE_TURNS

        def run(engine, step):
            def at(turn, c):
                def tile(k):
                    t = Tile(turn, c + k)
                    return t if not t.static or 0 <= t.index < TILES else None
                return tile
            for c in range(-DENSE_AHEAD, LOOP_FROM):
                step(at(0, c))
            with engine.Fori(0, TURNS) as turn:
                for c in range(LOOP_FROM, LOOP_FROM + UNROLL):
                    step(at(turn, c))
            for c in range(LOOP_FROM + TURNS * UNROLL, TILES + 1):
                step(at(0, c))

        def is_last(t):
            return t.static and t.index == TILES - 1

        with nc.Block(name="dense") as block:
            @block.sync
            def _(sp):
                def step(at):
                    if t := at(-1):
                        after(sp, result_done, t)
                        if is_last(t):
                            sp.dma_start(out[s.N - s.LAST_NEW:s.N, :], result[P - s.LAST_NEW:P, t.slot(MID), :])\
                                .then_inc(stored[t.slot(MID)], 16)
                        else:
                            sp.dma_start(out[bass.ds(t.index * P, P), :], result[:, t.slot(MID), :])\
                                .then_inc(stored[t.slot(MID)], 16)
                    if t := at(5):
                        after(sp, base_done, t, LONG)
                        first = s.LAST_BASE if is_last(t) else t.index * P
                        sp.dma_start(own[:, t.slot(LONG), :], x[bass.ds(first, P), :])\
                            .then_inc(own_in[t.slot(LONG)], 16)

                run(sp, step)
                for n in range(max(0, TILES - MID), TILES):
                    t = Tile(0, n)
                    sp.wait_ge(stored[t.slot(MID)], 16 * t.nth(MID))

            @block.gpsimd
            def _(pool):
                pool.memset(power[:, :], -0.5).then_inc(power_set, 1)
                pool.memset(eps[:, :], EPS).then_inc(power_set, 1)
                pool.wait_ge(power_set, 2)

                last_record = pool.alloc_register("last_record")
                pool.reg_mov(last_record, s.UNITS * P - 1)

                def send(half, j):
                    pool.indirect_dma_start(
                        out=s.records[:, :], out_offset=bass.IndirectOffsetOnAxis(ap=address[:, half, j:j + 1], axis=0),
                        in_=parcels[:, half, j, :], in_offset=None, bounds_check=last_record, oob_is_err=False)\
                        .then_inc(records_sent[half], 16)

                def step(at):
                    if parcel := parcel_of(at):
                        turn, half, third = parcel
                        if third == 0:
                            column = (turn + 1) * (2 * SENDS) + half * SENDS
                            if not isinstance(turn, int):
                                pool.wait_ge(records_sent[half], (turn + 1) * (16 * SENDS))
                            pool.tensor_copy(parcels[:, half, :, :], s.record[:, bass.ds(column, SENDS), :])\
                                .then_inc(parcel_ready[half], 1)
                            pool.tensor_copy(address[:, half, :], s.goes_to[:, bass.ds(column, SENDS)])\
                                .then_inc(parcel_ready[half], 1)
                            pool.wait_ge(parcel_ready[half], (turn + 2) * 2)
                    if t := at(2):
                        b = t.slot(LONG)
                        after(pool, moments_done, t)
                        pool.tensor_tensor(shifted[:, b:b + 1], moments[:, b, 1:2], eps[:, :], ALU.add)\
                            .then_inc(shifted_done, 1)
                        after(pool, shifted_done, t)
                        pool.tensor_tensor(norm[:, b, 0:1], shifted[:, b:b + 1], power[:, :], ALU.pow)\
                            .then_inc(rstd_done, 1)
                    if parcel:
                        for j in range(third * SENDS // 3, (third + 1) * SENDS // 3):
                            send(half, j)

                def parcel_of(at):
                    t = at(2)
                    if t is None or t.static and t.index - 2 >= LOOP_FROM:
                        return None
                    turn, sixth = (-1, t.c - 2 - LOOP_FROM + UNROLL) if t.static else (t.turn, t.c - 2 - LOOP_FROM)
                    return (turn, *divmod(sixth, UNROLL // 2))

                run(pool, step)
                for half in range(2):
                    pool.wait_ge(records_sent[half], 16 * SENDS * (TURNS + 1))

            @block.scalar
            def _(act):
                def step(at):
                    if t := at(1):
                        after(act, h_turned, t)
                        after(act, out_ready, t, SHORT)
                        act.activation(turned[:, t.slot(SHORT), 0], h_banks[t.slot(2)][:, :], ACT.Copy, scale=SCALE)\
                            .then_inc(h_hi_done, 1)
                    if t := at(2):
                        b, d = t.slot(LONG), t.slot(SHORT)
                        after(act, shift_done, t)
                        after(act, h_turned, t, SHORT)
                        act.activation(h[:, d, :], own[:, b, :], ACT.Relu, bias=norm[:, b, 1:2],
                                       scale=norm[:, b, 0:1]).then_inc(h_done, 1)

                run(act, step)

            @block.vector
            def _(dve):
                def step(at):
                    if t := at(-1):
                        after(dve, base_done, t)
                        after(dve, out_ready, t)
                        dve.scalar_tensor_tensor(result[:, t.slot(MID), :], out_banks[t.slot(2)][:, :], fold[:, :],
                                                 result[:, t.slot(MID), :], ALU.mult, ALU.add)\
                            .then_inc(result_done, 1)
                    if t := at(0):
                        d = t.slot(SHORT)
                        after(dve, h_hi_done, t)
                        dve.scalar_tensor_tensor(turned[:, d, 1], h_banks[t.slot(2)][:, :], SCALE, turned[:, d, 0],
                                                 ALU.mult, ALU.subtract).then_inc(h_lo_done, 1)
                    if t := at(3):
                        dve.wait_ge(own_in[t.slot(LONG)], 16 * t.nth(LONG))
                        dve.bn_stats(stats[:, t.slot(SHORT), :], own[:, t.slot(LONG), :]).then_inc(stats_done, 1)
                    if t := at(2):
                        b = t.slot(LONG)
                        after(dve, rstd_done, t)
                        dve.scalar_tensor_tensor(norm[:, b, 1:2], moments[:, b, 0:1], -1.0, norm[:, b, 0:1],
                                                 ALU.mult, ALU.mult).then_inc(shift_done, 1)
                    if t := at(0):
                        if at(3):
                            after(dve, stats_done, at(3))
                        if not t.static or t.index >= MID:
                            dve.wait_ge(stored[t.slot(MID)], 16 * (t.nth(MID) - 1))
                        dve.tensor_tensor(result[:, t.slot(MID), :], bias[:, :], own[:, t.slot(LONG), :], ALU.add)\
                            .then_inc(base_done, 1)
                    if t := at(3):
                        if t.static:
                            after(dve, stats_done, t)
                        dve.bn_aggr(moments[:, t.slot(LONG), :], stats[:, t.slot(SHORT), :]).then_inc(moments_done, 1)

                run(dve, step)

            @block.tensor
            def _(pe):
                def step(at):
                    if t := at(0):
                        d = t.slot(SHORT)
                        after(pe, h_hi_done, t)
                        after(pe, result_done, t, 2)
                        for f in range(FC):
                            for part in range(2):
                                pe.matmul(out_banks[t.slot(2)][:, :], turned[:, d, 0, f, :], weights[:, 0, part, f, :],
                                          start=(f == part == 0), stop=False)
                    if t := at(1):
                        after(pe, h_done, t)
                        after(pe, h_lo_done, t, 2)
                        for f in range(FC):
                            last = pe.transpose(h_banks[t.slot(2)][:, f * P:(f + 1) * P],
                                                h[:, t.slot(SHORT), f * P:(f + 1) * P], s.ident[:, :])
                        last.then_inc(h_turned, 1)
                    if t := at(0):
                        after(pe, h_lo_done, t)
                        for f in range(FC):
                            last = pe.matmul(out_banks[t.slot(2)][:, :], turned[:, d, 1, f, :], weights[:, 0, 0, f, :],
                                             start=False, stop=(f == FC - 1))
                        last.then_inc(out_ready, 1)

                run(pe, step)


def correct(nc, s):
    x, out, D, FC = s.x, s.out, s.D, s.FC
    weights, fold, banks = s.weights, s.fold, s.banks
    with ExitStack() as ctx:
        def sb(name, shape, dt):
            return ctx.enter_context(nc.sbuf_tensor(name, shape, dt))

        def sem(name):
            return ctx.enter_context(nc.semaphore(name))

        edge = sb("c_edge", [P, LONG, 4], i32)
        edge_f = sb("c_edge_f", [P, LONG, 2], fp32)
        share = sb("c_share", [P, LONG, 1], fp32)
        rows = sb("c_rows", [P, LONG, 2, D], fp32)
        same = sb("c_same", [P, LONG, P], fp32)
        scrap = sb("c_scrap", [P, LONG, P], fp32)
        before = sb("c_before", [P, LONG, 1], fp32)
        target = sb("c_target", [P, LONG, 1], i32)
        stats = sb("c_stats", [P, SHORT, 2, 6], fp32)
        moments = sb("c_moments", [P, LONG, 2, 2], fp32)
        shifted = sb("c_shifted", [P, LONG, 2], fp32)
        norm = sb("c_norm", [P, LONG, 2, 2], fp32)
        norm_in = sb("c_norm_in", [P, LONG, 2, 2], fp32)
        power = sb("c_power", [P, 2], fp32)
        h = sb("c_h", [P, SHORT, 2, D], fp32)
        diff = sb("c_diff", [P, MID, D], fp32)
        turned = sb("c_turned", [P, SHORT, 2, FC, P], fp16)
        addend = sb("c_addend", [P, MID, D], fp32)

        dst_banks, sum_banks, out_banks = banks[0:2], banks[2:4], banks[4:6]

        edge_in = [sem(f"c_edge_in{i}") for i in range(LONG)]
        rows_in = [sem(f"c_rows_in{i}") for i in range(LONG)]
        added, power_set = sem("c_added"), sem("c_power_set")
        drained = sem("c_drained")
        edge_f_done, share_done, same_done, before_done, target_done = (
            sem("c_edge_f"), sem("c_share_done"), sem("c_same_done"), sem("c_before_done"), sem("c_target_done"))
        stats_done, moments_done, shift_done, norm_in_done = (
            sem("c_stats_done"), sem("c_moments_done"), sem("c_shift_done"), sem("c_norm_in_done"))
        diff_done, sum_lo_done = sem("c_diff_done"), sem("c_sum_lo_done")
        shifted_done, rstd_done = sem("c_shifted_done"), sem("c_rstd_done")
        h_done, sum_hi_done, addend_done = sem("c_h_done"), sem("c_sum_hi_done"), sem("c_addend_done")
        dst_spread, summed, out_ready = sem("c_dst_spread"), sem("c_summed"), sem("c_out_ready")

        def run(engine, step):
            def at(turn, c):
                def unit(k):
                    t = Tile(turn, c + k)
                    return t if not t.static or t.index >= 0 else None
                return unit
            for c in range(-UNITS_AHEAD, LOOP_FROM):
                step(at(0, c))
            turns = engine.snap(engine.value_load(s.turns[0:1, 0:1], min_val=1, max_val=s.MAX_TURNS),
                                min_val=1, max_val=s.MAX_TURNS)
            with engine.Fori(0, turns) as turn:
                for c in range(LOOP_FROM, LOOP_FROM + UNROLL):
                    step(at(turn, c))
            return at(turns, LOOP_FROM - 1)

        with nc.Block(name="correct") as block:
            @block.sync
            def _(sp):
                def step(at):
                    if t := at(8):
                        after(sp, h_done, t, LONG)
                        sp.dma_start(edge[:, t.slot(LONG), :], s.records[bass.ds(t.index * P, P), :])\
                            .then_inc(edge_in[t.slot(LONG)], 16)

                run(sp, step)

            @block.gpsimd
            def _(pool):
                pool.memset(power[:, :], -0.5).then_inc(power_set, 1)
                pool.memset(rows[:, :, :, :], 0.0).then_inc(power_set, 1)
                pool.wait_ge(power_set, 2)

                last_row = pool.alloc_register("c_last_row")
                pool.reg_mov(last_row, s.N - 1)
                steps_over = pool.alloc_register("c_steps_over")
                pool.reg_mov(steps_over, 0)

                def step(at):
                    g, n, a = at(7), at(4), at(-2)
                    if g:
                        pool.wait_ge(edge_in[g.slot(LONG)], 16 * g.nth(LONG))
                        after(pool, h_done, g, LONG)
                    if n:
                        b = n.slot(LONG)
                        if a:
                            after(pool, addend_done, a)
                            after(pool, target_done, a)
                            after(pool, added, a, 1, by=16)
                        after(pool, shifted_done, n)
                        pool.tensor_tensor(norm[:, b, 0, :], shifted[:, b, :], power[:, :], ALU.pow)\
                            .then_inc(rstd_done, 1)
                    if a:
                        pool.indirect_dma_start(
                            out=out[:, :], out_offset=bass.IndirectOffsetOnAxis(ap=target[:, a.slot(LONG), :], axis=0),
                            in_=addend[:, a.slot(MID), :], in_offset=None, bounds_check=last_row, oob_is_err=False,
                            compute_op=ALU.add).then_inc(added, 16)
                    if g:
                        for k in range(2):
                            pool.indirect_dma_start(
                                out=rows[:, g.slot(LONG), k, :], out_offset=None, in_=x[:, :],
                                in_offset=bass.IndirectOffsetOnAxis(ap=edge[:, g.slot(LONG), k:k + 1], axis=0),
                                bounds_check=last_row, oob_is_err=False).then_inc(rows_in[g.slot(LONG)], 16)

                at = run(pool, step)
                after(pool, added, at(-2), by=16)
                pool.reg_add(steps_over, steps_over, 1)
                pool.wait_ge(rows_in[at(7).slot(LONG)], 32 * at(7).nth(LONG))
                pool.reg_add(steps_over, steps_over, 1)
                pool.wait_ge(edge_in[at(8).slot(LONG)], 16 * at(8).nth(LONG))
                pool.reg_add(steps_over, steps_over, 1)

            @block.scalar
            def _(act):
                def step(at):
                    if t := at(-1):
                        after(act, out_ready, t)
                        after(act, added, t, MID, by=16)
                        act.activation(addend[:, t.slot(MID), :], out_banks[t.slot(2)][:, :], ACT.Copy,
                                       scale=fold[:, :]).then_inc(addend_done, 1)
                    if t := at(1):
                        after(act, summed, t)
                        after(act, out_ready, t, SHORT)
                        act.activation(turned[:, t.slot(SHORT), 0], sum_banks[t.slot(2)][:, :], ACT.Copy)\
                            .then_inc(sum_hi_done, 1)
                    if t := at(4):
                        b, d = t.slot(LONG), t.slot(SHORT)
                        after(act, norm_in_done, t)
                        after(act, diff_done, t, SHORT)
                        for k in range(2):
                            last = act.activation(h[:, d, k, :], rows[:, b, k, :], ACT.Relu,
                                                  bias=norm_in[:, b, 1, k:k + 1], scale=norm_in[:, b, 0, k:k + 1])
                        last.then_inc(h_done, 1)

                run(act, step)

            @block.vector
            def _(dve):
                dve.wait_ge(power_set, 2)

                def step(at):
                    if t := at(5):
                        b5, d5 = t.slot(LONG), t.slot(SHORT)
                        after(dve, edge_f_done, t)
                        dve.reciprocal(share[:, b5, :], edge_f[:, b5, 1:2]).then_inc(share_done, 1)
                    if t := at(5):
                        dve.wait_ge(rows_in[b5], 32 * t.nth(LONG))
                        dve.bn_stats(stats[:, d5, 0, :], rows[:, b5, 0, :])
                        dve.bn_stats(stats[:, d5, 1, :], rows[:, b5, 1, :]).then_inc(stats_done, 1)
                    if t := at(0):
                        d = t.slot(SHORT)
                        after(dve, sum_hi_done, t)
                        if at(5):
                            after(dve, stats_done, at(5))
                        dve.tensor_tensor(turned[:, d, 1], sum_banks[t.slot(2)][:, :], turned[:, d, 0],
                                          ALU.subtract).then_inc(sum_lo_done, 1)
                    if t := at(5):
                        if t.static:
                            after(dve, stats_done, t)
                        dve.bn_aggr(moments[:, b5, 0, :], stats[:, d5, 0, :])
                        dve.bn_aggr(moments[:, b5, 1, :], stats[:, d5, 1, :]).then_inc(moments_done, 1)
                    if t := at(4):
                        b = t.slot(LONG)
                        after(dve, dst_spread, t)
                        after(dve, summed, t, LONG)
                        dve.tensor_scalar(same[:, b, :], dst_banks[t.slot(2)][:, 0:P], edge_f[:, b, 0:1], None,
                                          ALU.is_equal).then_inc(same_done, 1)
                    if t := at(5):
                        after(dve, moments_done, t)
                        dve.tensor_scalar(shifted[:, b5, :], moments[:, b5, :, 1], EPS, None, ALU.add)\
                            .then_inc(shifted_done, 1)
                    if t := at(4):
                        after(dve, rstd_done, t)
                        dve.scalar_tensor_tensor(norm[:, b, 1, :], moments[:, b, :, 0], -1.0, norm[:, b, 0, :],
                                                 ALU.mult, ALU.mult).then_inc(shift_done, 1)
                    if t := at(6):
                        dve.wait_ge(edge_in[t.slot(LONG)], 16 * t.nth(LONG))
                        after(dve, target_done, t, LONG)
                        dve.tensor_copy(edge_f[:, t.slot(LONG), :], edge[:, t.slot(LONG), 1:3]).then_inc(edge_f_done, 1)
                    if t := at(4):
                        after(dve, shift_done, t)
                        after(dve, share_done, t)
                        dve.tensor_scalar(norm_in[:, b, :, :], norm[:, b, :, :], share[:, b, :], SCALE,
                                          ALU.mult, ALU.mult).then_inc(norm_in_done, 1)
                    if t := at(3):
                        d = t.slot(SHORT)
                        after(dve, h_done, t)
                        after(dve, summed, t, MID)
                        dve.tensor_tensor(diff[:, t.slot(MID), :], h[:, d, 0, :], h[:, d, 1, :], ALU.subtract)\
                            .then_inc(diff_done, 1)
                    if t := at(4):
                        after(dve, same_done, t)
                        dve.tensor_tensor_reduce(out=scrap[:, b, :], in0=same[:, b, :], in1=s.lower[:, :], scale=1.0,
                                                 scalar=0.0, op0=ALU.mult, op1=ALU.add,
                                                 accum_out=before[:, b, :]).then_inc(before_done, 1)
                    if t := at(2):
                        b2 = t.slot(LONG)
                        after(dve, before_done, t)
                        after(dve, added, t, LONG, by=16)
                        dve.scalar_tensor_tensor(target[:, b2, :], before[:, b2, :], FAR, edge_f[:, b2, 0:1],
                                                 ALU.mult, ALU.add).then_inc(target_done, 1)

                run(dve, step)

            @block.tensor
            def _(pe):
                def step(at):
                    if t := at(1):
                        b, d = t.slot(LONG), t.slot(SHORT)
                        after(pe, same_done, t)
                        after(pe, diff_done, t)
                        after(pe, sum_lo_done, t, 2)
                        for f in range(FC):
                            c = slice(f * P, (f + 1) * P)
                            last = pe.matmul(sum_banks[t.slot(2)][:, c], diff[:, t.slot(MID), c], same[:, b, :],
                                             start=True, stop=True)
                        last.then_inc(summed, 1)
                    if t := at(0):
                        d = t.slot(SHORT)
                        after(pe, sum_hi_done, t)
                        after(pe, addend_done, t, 2)
                        for f in range(FC):
                            for part in range(2):
                                pe.matmul(out_banks[t.slot(2)][:, :], turned[:, d, 0, f, :], weights[:, 1, part, f, :],
                                          start=(f == part == 0), stop=False)
                    if t := at(5):
                        b = t.slot(LONG)
                        after(pe, edge_f_done, t)
                        after(pe, same_done, t, 2)
                        pe.matmul(dst_banks[t.slot(2)][:, 0:P], edge_f[:, b, 0:1].broadcast_to([P, P]), s.ident[:, :],
                                  start=True, stop=True).then_inc(dst_spread, 1)
                    if t := at(0):
                        after(pe, sum_lo_done, t)
                        for f in range(FC):
                            last = pe.matmul(out_banks[t.slot(2)][:, :], turned[:, d, 1, f, :], weights[:, 1, 0, f, :],
                                             start=False, stop=(f == FC - 1))
                        last.then_inc(out_ready, 1)

                run(pe, step)


def ranges(nc, s):
    E, EG, COLS, NSUB, ROW, TG, TCOLS, LAST_BASE = s.E, s.EG, s.COLS, s.NSUB, s.ROW, s.TG, s.TCOLS, s.LAST_BASE
    ident, ones, table, src_of, tinfo, banks = s.ident, s.ones, s.table, s.src_of, s.tinfo, s.banks
    with ExitStack() as ctx:
        def sb(name, shape, dt):
            return ctx.enter_context(nc.sbuf_tensor(name, shape, dt))

        def sem(name):
            return ctx.enter_context(nc.semaphore(name))

        raw_dst = sb("r_dst", [P, EG, P], i32)
        raw_src = sb("r_src", [P, EG, P], i32)
        cut = sb("r_cut", [P, 2, EG, P], i32)
        edge = sb("r_edge", [P, 4, EG, P], fp32)
        subs = sb("r_subs", [P, 2, EG * NSUB], fp32)
        diag = sb("r_diag", [P, 2, 4, P], fp32)
        rows = sb("r_rows", [P, 2, ROW], fp32)
        end_id = sb("r_end_id", [P, ROW], fp32)
        rev_id = sb("r_rev_id", [P, ROW], fp32)
        meet = sb("r_meet", [P, ROW], fp32)
        scrap = sb("r_scrap", [P, ROW], fp32)
        base_col = sb("r_base_col", [P, TG, 2], fp32)
        found = sb("r_found", [P, TG, 2], fp32)
        info = sb("r_info", [P, 3, TG], fp32)

        e_filled, e_in, consts, dve_done = sem("r_e_filled"), sem("r_e_in"), sem("r_consts"), sem("r_dve_done")
        edge_ready, edge_turned, edge_taken = sem("r_edge_ready"), sem("r_edge_turned"), sem("r_edge_taken")
        diag_ready, row_ready, row_taken = sem("r_diag_ready"), sem("r_row_ready"), sem("r_row_taken")

        full, rest = E // P, E % P
        edge_loads = []
        for raw, flat in ((raw_dst, s.dst), (raw_src, s.src)):
            for g in range(EG):
                n = min(P, full - g * P)
                if n > 0:
                    edge_loads.append((raw[0:n, g, :], flat[g * P * P:(g * P + n) * P].rearrange("(q e) -> q e", e=P)))
            if rest:
                q = full % P
                edge_loads.append((raw[q:q + 1, full // P, 0:rest], flat[full * P:E].rearrange("(a e) -> a e", a=1)))

        def needed(engine):
            return engine.If(engine.value_load(s.n_bad[0:1, 0:1], min_val=0, max_val=4 * E) > 0)

        with nc.Block(name="ranges") as block:
            @block.sync
            def _(sp):
                with needed(sp):
                    sp.wait_ge(e_filled, 2)
                    for to, frm in edge_loads:
                        sp.dma_start(to, frm).then_inc(e_in, 16)

            @block.gpsimd
            def _(pool):
                with needed(pool):
                    pool.memset(raw_dst[:, :, :], int(FAR)).then_inc(e_filled, 1)
                    pool.memset(raw_src[:, :, :], 0).then_inc(e_filled, 1)
                    pool.iota(base_col[:, :, 0], pattern=[[P * P, TG]], base=0, channel_multiplier=P,
                              allow_small_or_imprecise_dtypes=True).then_inc(consts, 1)
                    pool.iota(end_id[:, :], pattern=[[P, EG], [0, NSUB], [1, P]], base=1, channel_multiplier=0,
                              allow_small_or_imprecise_dtypes=True).then_inc(consts, 1)

            @block.vector
            def _(dve):
                step = [0]

                def link(ins):
                    step[0] += 1
                    ins.then_inc(dve_done, 1)
                    dve.wait_ge(dve_done, step[0])

                def table_of_edges():
                    dve.wait_ge(consts, 2)
                    dve.wait_ge(e_in, 16 * len(edge_loads))
                    dve.tensor_copy(edge[:, 0, :, :], raw_dst[:, :, :])
                    link(dve.tensor_copy(edge[:, 2, :, :], raw_src[:, :, :]))
                    link(dve.tensor_tensor(edge[:, 1, :, :], edge[:, 0, :, :], edge[:, 2, :, :], ALU.not_equal))
                    dve.tensor_scalar(cut[:, 0, :, :], raw_src[:, :, :], 8, None, ALU.logical_shift_right)
                    link(dve.tensor_scalar(cut[:, 1, :, :], raw_src[:, :, :], 255, None, ALU.bitwise_and))
                    dve.tensor_scalar(edge[:, 2, :, :], cut[:, 0, :, :], -512.0, None, ALU.add)
                    dve.tensor_copy(edge[:, 3, :, :], cut[:, 1, :, :]).then_inc(edge_ready, 1)
                    for g in range(EG):
                        dve.wait_ge(edge_turned, g + 1)
                        dve.tensor_copy(table[:, g * P:(g + 1) * P, 0:4],
                                        banks[2 + g % 2].rearrange("p (k q) -> p q k", k=4)).then_inc(edge_taken, 1)
                    dve.wait_ge(edge_taken, EG)
                    link(dve.tensor_scalar(scrap[:, 0:COLS], table[:, 0:COLS, 2], 512.0, 256.0, ALU.add, ALU.mult))
                    dve.tensor_tensor(src_of[:, :], scrap[:, 0:COLS], table[:, 0:COLS, 3], ALU.add)

                turns = [0]

                def row_turn(columns, take):
                    n = turns[0]
                    if n >= 2:
                        dve.wait_ge(row_ready, n - 1)
                    for k, column in enumerate(columns):
                        ins = dve.tensor_scalar(diag[:, n % 2, k, :], ident[:, :], column, None, ALU.mult)
                    ins.then_inc(diag_ready, 1)
                    dve.wait_ge(row_ready, n + 1)
                    take(banks[n % 2]).then_inc(row_taken, 1)
                    turns[0] += 1

                with needed(dve):
                    table_of_edges()
                    by_sub = edge[:, 0, :, :].rearrange("p g (s e) -> p (g s) e", e=SUB)
                    dve.tensor_reduce(subs[:, 0, :], by_sub, AX.X, ALU.min)
                    link(dve.tensor_reduce(subs[:, 1, :], by_sub, AX.X, ALU.max))
                    link(dve.tensor_scalar(base_col[:, :, 0], base_col[:, :, 0], float(LAST_BASE), None, ALU.min))
                    dve.tensor_scalar(base_col[:, :, 1], base_col[:, :, 0], float(P), None, ALU.add)
                    link(dve.tensor_scalar(rev_id[:, :], end_id[:, :], -1.0, float(COLS + 1), ALU.mult, ALU.add))
                    flat_subs, flat_rows = (subs[:, :, :].rearrange("p k c -> p (k c)"),
                                            rows[:, :, :].rearrange("p k c -> p (k c)"))
                    for c in range(0, 2 * EG * NSUB, 4):
                        w = min(4, 2 * EG * NSUB - c)
                        row_turn([flat_subs[:, c + i:c + i + 1] for i in range(w)],
                                 lambda bank: dve.tensor_copy(flat_rows[:, c * P:(c + w) * P], bank[:, 0:w * P]))
                    link(dve.memset(found[:, :, :], 0.0))
                    for g in range(TG):
                        link(dve.tensor_scalar(meet[:, :], rows[:, 1, :], base_col[:, g, 0:1], None, ALU.is_ge))
                        link(dve.scalar_tensor_tensor(meet[:, :], rows[:, 0, :], base_col[:, g, 1:2], meet[:, :],
                                                      ALU.is_lt, ALU.mult))
                        for k, weight in enumerate((rev_id[:, :], end_id[:, :])):
                            link(dve.tensor_tensor_reduce(out=scrap[:, :], in0=meet[:, :], in1=weight, scale=1.0,
                                                          scalar=0.0, op0=ALU.mult, op1=ALU.max,
                                                          accum_out=found[:, g, k:k + 1]))
                    link(dve.tensor_scalar(info[:, 0, :], found[:, :, 0], -1.0, float(COLS), ALU.mult, ALU.add))
                    link(dve.tensor_scalar(info[:, 0, :], info[:, 0, :], float(COLS - 1), None, ALU.min))
                    link(dve.scalar_tensor_tensor(info[:, 1, :], info[:, 0, :], 1.0, found[:, :, 1], ALU.add, ALU.max))
                    link(dve.tensor_copy(info[:, 2, :], base_col[:, :, 0]))
                    for k in range(3):
                        for c in range(0, TG, 4):
                            w = min(4, TG - c)
                            row_turn([info[:, k, c + i:c + i + 1] for i in range(w)],
                                     lambda bank: dve.tensor_copy(tinfo[:, k, c * P:(c + w) * P], bank[:, 0:w * P]))

            @block.tensor
            def _(pe):
                with needed(pe):
                    pe.wait_ge(edge_ready, 1)
                    for g in range(EG):
                        if g >= 2:
                            pe.wait_ge(edge_taken, g - 1)
                        for k in range(4):
                            last = pe.transpose(banks[2 + g % 2][:, k * P:(k + 1) * P], edge[:, k, g, :], ident[:, :])
                        last.then_inc(edge_turned, 1)
                    widths = ([min(4, 2 * EG * NSUB - c) for c in range(0, 2 * EG * NSUB, 4)]
                              + 3 * [min(4, TG - c) for c in range(0, TG, 4)])
                    for n, width in enumerate(widths):
                        pe.wait_ge(diag_ready, n + 1)
                        if n >= 2:
                            pe.wait_ge(row_taken, n - 1)
                        pe.matmul(banks[n % 2][:, 0:width * P], ones[:, :], diag[:, n % 2, 0:width, :],
                                  start=True, stop=True).then_inc(row_ready, 1)


def general(nc, s):
    x, out, D, FC, TILES = s.x, s.out, s.D, s.FC, s.TILES
    ident, ones16, from0 = s.ident, s.ones16, s.from0
    weights, fold, table, tinfo, banks = s.weights, s.fold, s.table, s.tinfo, s.banks
    with ExitStack() as ctx:
        def sb(name, shape, dt):
            return ctx.enter_context(nc.sbuf_tensor(name, shape, dt))

        def sem(name):
            return ctx.enter_context(nc.semaphore(name))

        own = sb("g_own", [P, D], fp32)
        far = sb("g_far", [P, D], fp32)
        result = sb("g_result", [P, D], fp32)
        row_id = sb("g_row_id", [P, 1], i32)
        base = sb("g_base", [P, 1], fp32)
        local = sb("g_local", [P, 1], fp32)
        to_node = sb("g_to_node", [P, P], fp16)
        zeros = sb("g_zeros", [P, D], fp16)
        stats = sb("g_stats", [P, 6], fp32)
        moments = sb("g_moments", [P, 2], fp32)
        shifted = sb("g_shifted", [P, 1], fp32)
        power = sb("g_power", [P, 1], fp32)
        eps = sb("g_eps", [P, 1], fp32)
        rstd = sb("g_rstd", [P, 1], fp32)
        shift = sb("g_shift", [P, 1], fp32)
        h = sb("g_h", [P, D], fp32)
        h_hi = sb("g_h_hi", [P, D], fp16)
        h_lo = sb("g_h_lo", [P, D], fp16)
        inverse = sb("g_inverse", [P, P], fp32)
        mean = sb("g_mean", [P, FC, P], fp32)
        has_edge = sb("g_has_edge", [P, 1], fp32)
        turned = sb("g_turned", [P, 2, 2, FC, P], fp16)
        h_bank, mean_bank, degree_bank, out_bank = banks[0:4]

        own_in, far_in, stored = sem("g_own_in"), sem("g_far_in"), sem("g_stored")
        pool_own, dve_own = sem("g_pool_own"), sem("g_dve_own")
        set_up = sem("g_set_up")
        moments_done, rstd_done, item_ready, item_used = (
            sem("g_moments"), sem("g_rstd"), sem("g_item_ready"), sem("g_item_used"))
        mean_split, out_ready, result_done = sem("g_mean_split"), sem("g_out_ready"), sem("g_result_done")

        class Count:

            def __init__(self, engine, name):
                self.engine, self.reg = engine, engine.alloc_register(name)
                engine.reg_mov(self.reg, 0)

            def value(self):
                return self.engine.snap(self.reg)

            def add(self):
                self.engine.reg_add(self.reg, self.reg, 1)

        def tile_by_tile(engine, own_part, chunk_part, tile_part):
            with engine.If(engine.value_load(s.n_bad[0:1, 0:1], min_val=0, max_val=4 * s.E) > 0):
                with engine.Fori(0, TILES) as t:
                    own_part(t)
                    first = engine.value_load(tinfo[0:1, 0, bass.ds(t, 1)], min_val=0, max_val=s.COLS)
                    end = engine.value_load(tinfo[0:1, 1, bass.ds(t, 1)], min_val=0, max_val=s.COLS)
                    with engine.Fori(first, end) as chunk:
                        chunk_part(engine.snap(chunk, min_val=0, max_val=s.COLS - 1))
                    tile_part(t)

        with nc.Block(name="general") as block:
            @block.gpsimd
            def _(pool):
                items, tiles, chunks, own_steps = (Count(pool, "pool_items"), Count(pool, "pool_tiles"),
                                                   Count(pool, "pool_chunks"), Count(pool, "pool_steps"))
                pool.memset(power[:, :], -0.5).then_inc(set_up, 1)
                pool.memset(eps[:, :], EPS).then_inc(set_up, 1)
                pool.memset(zeros[:, :], 0.0).then_inc(set_up, 1)
                pool.wait_ge(set_up, 3)

                last_row = pool.alloc_register("g_last_row")
                pool.reg_mov(last_row, s.N - 1)

                def own_step(ins):
                    ins.then_inc(pool_own, 1)
                    pool.wait_ge(pool_own, own_steps.value() + 1)
                    own_steps.add()

                def normalise():
                    pool.wait_ge(moments_done, items.value() + 1)
                    own_step(pool.tensor_tensor(shifted[:, :], moments[:, 1:2], eps[:, :], ALU.add))
                    pool.tensor_tensor(rstd[:, :], shifted[:, :], power[:, :], ALU.pow).then_inc(rstd_done, 1)
                    pool.wait_ge(item_used, items.value() + 1)
                    items.add()

                def own_part(t):
                    first = pool.value_load(tinfo[0:1, 2, bass.ds(t, 1)], min_val=0, max_val=s.LAST_BASE)
                    pool.dma_start(own[:, :], x[bass.ds(first, P), :]).then_inc(own_in, 16)
                    normalise()

                def chunk_part(chunk):
                    own_step(pool.tensor_copy(row_id[:, :], s.src_of[:, bass.ds(chunk, 1)]))
                    pool.indirect_dma_start(
                        out=far[:, :], out_offset=None, in_=x[:, :],
                        in_offset=bass.IndirectOffsetOnAxis(ap=row_id[:, :], axis=0),
                        bounds_check=last_row, oob_is_err=False).then_inc(far_in, 16)
                    normalise()

                def tile_part(t):
                    pool.wait_ge(result_done, tiles.value() + 1)
                    tiles.add()
                    first = pool.value_load(tinfo[0:1, 2, bass.ds(t, 1)], min_val=0, max_val=s.LAST_BASE)
                    pool.dma_start(out[bass.ds(first, P), :], result[:, :]).then_inc(stored, 16)
                    pool.wait_ge(stored, tiles.value() * 16)

                tile_by_tile(pool, own_part, chunk_part, tile_part)

            @block.vector
            def _(dve):
                items, tiles, chunks, own_steps = (Count(dve, "dve_items"), Count(dve, "dve_tiles"),
                                                   Count(dve, "dve_chunks"), Count(dve, "dve_steps"))

                def own_step(ins):
                    ins.then_inc(dve_own, 1)
                    own_steps.add()
                    dve.wait_ge(dve_own, own_steps.value())

                def normalise(rows, meanwhile):
                    own_step(dve.bn_stats(stats[:, :], rows))
                    meanwhile()
                    dve.bn_aggr(moments[:, :], stats[:, :]).then_inc(moments_done, 1)
                    dve.wait_ge(rstd_done, items.value() + 1)
                    own_step(dve.scalar_tensor_tensor(shift[:, :], moments[:, 0:1], -1.0, rstd[:, :],
                                                      ALU.mult, ALU.mult))
                    own_step(dve.tensor_scalar(h[:, :], rows, rstd[:, :], shift[:, :], ALU.mult, ALU.add))

                def own_part(t):
                    dve.wait_ge(own_in, tiles.value() * 16 + 16)
                    normalise(own[:, :], lambda: dve.tensor_copy(base[:, :], tinfo[:, 2, bass.ds(t, 1)]))
                    dve.tensor_scalar(h[:, :], h[:, :], 0.0, None, ALU.max).then_inc(item_ready, 1)
                    dve.wait_ge(item_used, items.value() + 1)
                    own_step(dve.tensor_scalar(turned[:, 0, 0], h_bank[:, :], SCALE, None, ALU.mult))
                    own_step(dve.scalar_tensor_tensor(turned[:, 0, 1], h_bank[:, :], SCALE, turned[:, 0, 0],
                                                      ALU.mult, ALU.subtract))
                    items.add()

                def chunk_part(chunk):
                    dve.wait_ge(far_in, chunks.value() * 16 + 16)

                    def nodes():
                        own_step(dve.tensor_scalar(local[:, :], table[:, bass.ds(chunk, 1), 0], base[:, :], None,
                                                   ALU.subtract))
                        dve.tensor_scalar(to_node[:, :], from0[:, :], local[:, :], None, ALU.is_equal)

                    normalise(far[:, :], nodes)
                    own_step(dve.tensor_scalar(h[:, :], h[:, :], 0.0, SCALE, ALU.max, ALU.mult))
                    own_step(dve.tensor_copy(h_hi[:, :], h[:, :]))
                    dve.tensor_tensor(h_lo[:, :], h[:, :], h_hi[:, :], ALU.subtract).then_inc(item_ready, 1)
                    dve.wait_ge(item_used, items.value() + 1)
                    items.add()
                    chunks.add()

                def tile_part(t):
                    own_step(dve.tensor_scalar(inverse[:, :], degree_bank[:, 0:P], 1.0, None, ALU.max))
                    own_step(dve.reciprocal(inverse[:, :], inverse[:, :]))
                    own_step(dve.tensor_scalar(has_edge[:, :], degree_bank[:, P:P + 1], 1.0, None, ALU.min))
                    dve.scalar_tensor_tensor(result[:, :], s.bias[:, :], has_edge[:, :], own[:, :], ALU.mult, ALU.add)
                    for f in range(FC):
                        last = dve.tensor_tensor(mean[:, f, :], mean_bank[:, f * P:(f + 1) * P], inverse[:, :], ALU.mult)
                    own_step(last)
                    own_step(dve.scalar_tensor_tensor(mean[:, :, :], h_bank.rearrange("p (f n) -> p f n", f=FC), -SCALE,
                                                      mean[:, :, :], ALU.mult, ALU.add))
                    own_step(dve.tensor_copy(turned[:, 1, 0], mean[:, :, :]))
                    dve.tensor_tensor(turned[:, 1, 1], mean[:, :, :], turned[:, 1, 0], ALU.subtract)\
                        .then_inc(mean_split, 1)
                    dve.wait_ge(out_ready, tiles.value() + 1)
                    dve.scalar_tensor_tensor(result[:, :], out_bank[:, :], fold[:, :], result[:, :],
                                             ALU.mult, ALU.add).then_inc(result_done, 1)
                    tiles.add()

                dve.wait_ge(set_up, 3)
                tile_by_tile(dve, own_part, chunk_part, tile_part)

            @block.tensor
            def _(pe):
                items, tiles = Count(pe, "pe_items"), Count(pe, "pe_tiles")
                pe.wait_ge(set_up, 3)

                def own_part(t):
                    pe.wait_ge(item_ready, items.value() + 1)
                    for f in range(FC):
                        last = pe.transpose(h_bank[:, f * P:(f + 1) * P], h[:, f * P:(f + 1) * P], ident[:, :])
                    pe.matmul(mean_bank[:, :], zeros[:, 0:P], zeros[:, :], start=True, stop=False,
                              skip_group_check=True)
                    last = pe.matmul(degree_bank[:, 0:P + 1], zeros[:, 0:P], zeros[:, 0:P + 1], start=True, stop=False,
                                     skip_group_check=True)
                    last.then_inc(item_used, 1)
                    items.add()

                def chunk_part(chunk):
                    pe.wait_ge(item_ready, items.value() + 1)
                    for f in range(FC):
                        c = slice(f * P, (f + 1) * P)
                        for part in (h_hi, h_lo):
                            pe.matmul(mean_bank[:, c], part[:, c], to_node[:, :], start=False, stop=False,
                                      skip_group_check=True)
                    pe.matmul(degree_bank[:, 0:P], ones16[:, :], to_node[:, :], start=False, stop=False,
                              skip_group_check=True)
                    pe.matmul(degree_bank[:, P:P + 1], to_node[:, :], ones16[:, 0:1], start=False, stop=False,
                              skip_group_check=True).then_inc(item_used, 1)
                    items.add()

                def tile_part(t):
                    pe.wait_ge(mean_split, tiles.value() + 1)
                    for k in range(2):
                        for f in range(FC):
                            for hi_lo, part in ((0, 0), (0, 1), (1, 0)):
                                last = pe.matmul(out_bank[:, :], turned[:, k, hi_lo, f, :], weights[:, k, part, f, :],
                                                 start=(k == f == hi_lo == part == 0),
                                                 stop=(k == 1 and f == FC - 1 and hi_lo == 1))
                    last.then_inc(out_ready, 1)
                    tiles.add()

                tile_by_tile(pe, own_part, chunk_part, tile_part)


_INS = ["x", "src", "dst", "L0_gnn_W_l", "L0_gnn_b_l", "L0_gnn_W_r"]


def kernel(**inputs):
    import numpy as _np
    import concourse.bacc as _bacc
    from concourse import mybir as _mybir
    from concourse.bass_utils import run_bass_kernel_spmd as _run

    nc = _bacc.Bacc("TRN2", target_bir_lowering=False, num_devices=1)
    arrays, args = {}, []
    for name in _INS:
        a = _np.ascontiguousarray(inputs[name])
        arrays[f"in_{name}_dram"] = a
        args.append(nc.dram_tensor(f"in_{name}_dram", a.shape, _mybir.dt.from_np(a.dtype), kind="ExternalInput").ap())
    shape = arrays["in_x_dram"].shape
    out = nc.dram_tensor("out_0_dram", shape, _mybir.dt.float32, kind="ExternalOutput").ap()
    gnn_kernel(nc, *args, out)
    r = _run(nc, [arrays], core_ids=[0])
    return r.results[0]["out_0_dram"]
```

```python
from contextlib import ExitStack

import concourse.bass as bass
from concourse import mybir

P = 128
HALO = 16
SUB = 64
UNROLL = 6
LOOP_FROM = 4
DENSE_AHEAD = 5
UNITS_AHEAD = 9
LONG, MID, SHORT = 6, 3, 2
FAR = float(1 << 17)
SCALE = 256.0
EPS = 1e-5

fp32, fp16, i32 = mybir.dt.float32, mybir.dt.float16, mybir.dt.int32
ALU = mybir.AluOpType
ACT = mybir.ActivationFunctionType
AX = mybir.AxisListType
RMAX = bass.bass_isa.ReduceOp.max


class Shared:
    pass


class Tile:

    def __init__(self, turn, c):
        self.turn, self.c = turn, c
        self.index = turn * UNROLL + c
        self.static = isinstance(turn, int)

    def slot(self, depth):
        return self.c % depth

    def nth(self, depth):
        return self.turn * (UNROLL // depth) + self.c // depth + 1


def after(engine, semaphore, tile, lag=0, by=1):
    value = tile.index - lag + 1
    if tile.static and value <= 0:
        return
    engine.wait_ge(semaphore, value * by)


def gnn_kernel(nc, x, src, dst, w_l, b_l, w_r, out):
    N, D = x.shape
    E = src.shape[0]
    FC = D // P
    TILES = -(-N // P)
    LAST_BASE = N - P
    LAST_NEW = N - (TILES - 1) * P
    CHUNKS = -(-E // P)
    EG = -(-CHUNKS // P)
    COLS = EG * P
    NSUB = P // SUB
    ROW = EG * NSUB * P
    TG = -(-TILES // P)
    TCOLS = TG * P
    W = -(-E // P)
    DENSE_TURNS = (TILES - DENSE_AHEAD - LOOP_FROM) // UNROLL
    SENDS = -(-W // (2 * (DENSE_TURNS + 1)))
    RCOLS = SENDS * 2 * (DENSE_TURNS + 1)
    MAX_TURNS = -(-E // (UNROLL * P))
    UNITS = MAX_TURNS * UNROLL + LOOP_FROM + UNITS_AHEAD + 1
    assert W <= 2048 and MAX_TURNS <= P and UNITS * P <= FAR and N <= FAR and HALO <= W

    ctx = ExitStack()
    with ctx:
        def sb(name, shape, dt):
            return ctx.enter_context(nc.sbuf_tensor(name, shape, dt))

        ident = sb("ident", [P, P], fp32)
        ones = sb("ones", [P, P], fp32)
        ones16 = sb("ones16", [P, P], fp16)
        upper = sb("upper", [P, P], fp16)
        lower = sb("lower", [P, P], fp16)
        from0 = sb("from0", [P, P], fp32)
        weights = sb("weights", [P, 2, 2, FC, D], fp16)
        bias = sb("bias", [P, D], fp32)
        fold = sb("fold", [P, 1], fp32)
        record = sb("record", [P, RCOLS, 4], i32)
        goes_to = sb("goes_to", [P, RCOLS], i32)
        turns = sb("turns", [P, 1], i32)
        n_bad = sb("n_bad", [P, 1], i32)
        edge = sb("c_edge", [P, LONG, 4], i32)
        rows = sb("c_rows", [P, LONG, 2, D], fp32)
        records = nc.dram_tensor("records", [UNITS * P, 4], i32, kind="Internal").ap()

        banks = [ctx.enter_context(nc.psum_tensor(f"bank{i}", [P, 512], fp32)) for i in range(8)]

        s = Shared()
        s.x, s.src, s.dst, s.w_l, s.b_l, s.w_r, s.out = x, src, dst, w_l, b_l, w_r, out
        (s.N, s.D, s.E, s.FC, s.TILES, s.LAST_BASE, s.LAST_NEW, s.EG, s.COLS, s.NSUB, s.ROW, s.TG, s.TCOLS) = (
            N, D, E, FC, TILES, LAST_BASE, LAST_NEW, EG, COLS, NSUB, ROW, TG, TCOLS)
        s.W, s.DENSE_TURNS, s.SENDS, s.RCOLS, s.MAX_TURNS, s.UNITS = W, DENSE_TURNS, SENDS, RCOLS, MAX_TURNS, UNITS
        (s.ident, s.ones, s.ones16, s.upper, s.lower, s.from0) = (ident, ones, ones16, upper, lower, from0)
        (s.weights, s.bias, s.fold, s.record, s.goes_to, s.turns, s.n_bad, s.records, s.banks) = (
            weights, bias, fold, record, goes_to, turns, n_bad, records, banks)
        s.edge, s.rows = edge, rows
        prepare(nc, s)
        with ExitStack() as s.main, nc.Block(name="main") as block:
            dense(nc, s, block)
            correct(nc, s, block)
        table = sb("table", [P, COLS, 4], fp32)
        s.table = table
        s.src_of = sb("src_of", [P, COLS], i32)
        s.tinfo = sb("tinfo", [P, 3, TCOLS], i32)
        ranges(nc, s)
        general(nc, s)


def prepare(nc, s):
    D, E, N, FC, W, RCOLS = s.D, s.E, s.N, s.FC, s.W, s.RCOLS
    ident, ones, ones16, upper, lower, from0 = s.ident, s.ones, s.ones16, s.upper, s.lower, s.from0
    weights, bias, fold, record, goes_to, banks = s.weights, s.bias, s.fold, s.record, s.goes_to, s.banks
    L = W + 2 * HALO
    HERE = slice(HALO, HALO + W)
    STEPS = (W - 1).bit_length()
    PAD = 1 << (STEPS - 1)
    DOUBLINGS = (HALO - 1).bit_length()
    with ExitStack() as ctx:
        def sb(name, shape, dt):
            return ctx.enter_context(nc.sbuf_tensor(name, shape, dt))

        def sem(name):
            return ctx.enter_context(nc.semaphore(name))

        raw_w = sb("raw_w", [P, 2, FC, D], fp32)
        raw_dst = sb("raw_dst", [P, L], i32)
        raw_src = sb("raw_src", [P, W], i32)
        node = sb("node", [P, L], fp32)
        other = sb("other", [P, W], fp32)
        differs = sb("differs", [P, L], fp32)
        position = sb("position", [P, L], fp32)
        from_end = sb("from_end", [P, L], fp32)
        left = sb("left", [P, 2, L], fp32)
        right = sb("right", [P, 2, L], fp32)
        degree = sb("degree", [P, W], fp32)
        real = sb("real", [P, W], fp32)
        crowded = sb("crowded", [P, W], fp32)
        prefix = sb("prefix", [P, 3, PAD + W], fp32)
        sent = prefix[:, 2, PAD:]
        skip = sb("skip", [P, W], fp32)
        scrap = sb("scrap", [P, W], fp32)
        counts = sb("counts", [P, 4], fp32)
        counts16 = sb("counts16", [P, 4], fp16)
        totals = sb("totals", [P, 5], fp32)
        turn_starts = sb("turn_starts", [P, P], fp32)
        n_turns = sb("n_turns", [P, 1], fp32)
        bad = sb("bad", [P, 1], fp32)
        blank = sb("blank", [P, s.UNITS, 4], i32)
        wmax = sb("wmax", [P, 4], fp32)
        wint = sb("wint", [P, 2], i32)
        wscale = sb("wscale", [P, 1], fp32)

        wr_in, wl_in, b_in, e_in, blank_in = sem("wr_in"), sem("wl_in"), sem("b_in"), sem("e_in"), sem("blank_in")
        dst_filled, src_filled, blank_filled = sem("dst_filled"), sem("src_filled"), sem("blank_filled")
        pool_done, consts, padded, positions = sem("pool_done"), sem("consts"), sem("padded"), sem("positions")
        w_summed, wmax_ready, wmax_shared, wscale_ready = (
            sem("w_summed"), sem("wmax_ready"), sem("wmax_shared"), sem("wscale_ready"))
        dve_done = sem("dve_done")
        w_turned, w_hi, w_taken = sem("w_turned"), sem("w_hi"), sem("w_taken")
        sent_done, prefix_done = sem("sent_done"), sem("prefix_done")
        counted, totalled = sem("counted"), sem("totalled")

        def edge_loads(raw, flat, halo):
            span = W + 2 * halo
            inside = [p for p in range(P) if p * W - halo >= 0 and p * W - halo + span <= E]
            lo, hi = inside[0], inside[-1] + 1
            first = lo * W - halo
            loads = [(raw[lo:hi, :], bass.AP(flat.tensor, first, [[W, hi - lo], [1, span]]))]
            for p in range(P):
                a, b = max(p * W - halo, 0), min(p * W - halo + span, E)
                if not lo <= p < hi and a < b:
                    c = a - (p * W - halo)
                    loads.append((raw[p:p + 1, c:c + b - a], flat[a:b].rearrange("(a e) -> a e", a=1)))
            return loads

        loads = edge_loads(raw_dst, s.dst, HALO)
        dst_loads = len(loads)
        loads += edge_loads(raw_src, s.src, 0)

        with nc.Block(name="prepare") as block:
            @block.sync
            def _(sp):
                sp.wait_ge(dst_filled, 1)
                for n, (to, frm) in enumerate(loads):
                    if n == dst_loads:
                        sp.wait_ge(src_filled, 1)
                    sp.dma_start(to, frm).then_inc(e_in, 16)
                sp.dma_start(raw_w[:, 0, :, :], s.w_r.rearrange("(o p) f -> p o f", p=P)).then_inc(wr_in, 16)
                sp.dma_start(raw_w[:, 1, :, :], s.w_l.rearrange("(o p) f -> p o f", p=P)).then_inc(wl_in, 16)
                sp.dma_start(bias[:, :], s.b_l.rearrange("(a n) -> a n", a=1).broadcast_to([P, D])).then_inc(b_in, 16)
                sp.wait_ge(blank_filled, 3)
                sp.dma_start(s.records.rearrange("(p u) k -> p u k", p=P), blank[:, :, :]).then_inc(blank_in, 16)
                sp.wait_ge(b_in, 16)
                sp.wait_ge(blank_in, 16)

            @block.gpsimd
            def _(pool):
                step = [0]

                def link(ins):
                    step[0] += 1
                    ins.then_inc(pool_done, 1)
                    pool.wait_ge(pool_done, step[0])

                link(pool.memset(raw_dst[:, :], int(FAR)))
                pool.memset(raw_dst[0:1, 0:HALO], -5).then_inc(dst_filled, 1)
                pool.memset(raw_src[:, :], int(FAR)).then_inc(src_filled, 1)
                pool.memset(ones[:, :], 1.0)
                pool.memset(ones16[:, :], 1.0)
                link(pool.memset(ident[:, :], 0.0))
                link(pool.affine_select(out=ident[:, :], in_=ident[:, :], compare_op=ALU.not_equal, fill=1.0,
                                        base=0, pattern=[[-1, P]], channel_multiplier=1))
                link(pool.memset(upper[:, :], 1.0))
                pool.affine_select(out=upper[:, :], in_=upper[:, :], compare_op=ALU.is_gt, fill=0.0,
                                   base=0, pattern=[[1, P]], channel_multiplier=-1)
                link(pool.memset(lower[:, :], 1.0))
                link(pool.affine_select(out=lower[:, :], in_=lower[:, :], compare_op=ALU.is_gt, fill=0.0,
                                        base=0, pattern=[[-1, P]], channel_multiplier=1))
                pool.iota(from0[:, :], pattern=[[1, P]], base=0, channel_multiplier=0,
                          allow_small_or_imprecise_dtypes=True).then_inc(consts, 1)
                for k in range(3):
                    pool.memset(prefix[:, k, 0:PAD], 0.0).then_inc(padded, 1)
                pool.wait_ge(padded, 3)
                pool.iota(position[:, :], pattern=[[1, L]], base=0, channel_multiplier=0,
                          allow_small_or_imprecise_dtypes=True).then_inc(positions, 1)
                pool.iota(from_end[:, :], pattern=[[-1, L]], base=L, channel_multiplier=0,
                          allow_small_or_imprecise_dtypes=True).then_inc(positions, 1)
                pool.memset(s.rows[:, :, :, :], 0.0)
                pool.wait_ge(sent_done, 1)
                for k in range(STEPS):
                    a, b = (2 if k == 0 else 1 - k % 2), k % 2
                    last = pool.tensor_tensor(prefix[:, b, PAD:], prefix[:, a, PAD:],
                                              prefix[:, a, PAD - (1 << k):PAD + W - (1 << k)], ALU.add)
                    if k < STEPS - 1:
                        link(last)
                    if k == 2:
                        pool.wait_ge(wmax_ready, 1)
                        pool.partition_all_reduce(wmax[:, 3:4], wmax[:, 2:3], P, RMAX).then_inc(wmax_shared, 1)
                last.then_inc(prefix_done, 1)
                pool.memset(blank[:, :, 0:2], int(FAR)).then_inc(blank_filled, 1)
                pool.memset(blank[:, :, 2], 1).then_inc(blank_filled, 1)
                pool.memset(blank[:, :, 3], 0).then_inc(blank_filled, 1)
                if RCOLS > W:
                    pool.memset(goes_to[:, W:], int(FAR))
                    pool.memset(record[:, W:, 0:3], 0)
                pool.memset(record[:, :, 3], 0)
                pool.tensor_copy(record[:, 0:W, 0], raw_src[:, :])
                pool.tensor_copy(record[:, 0:W, 1], raw_dst[:, HERE])

            @block.scalar
            def _(act):
                act.wait_ge(wscale_ready, 1)
                for n in range(2 * FC):
                    k, f = 1 - n // FC, n % FC
                    act.wait_ge(w_turned, n + 1)
                    act.activation(weights[:, k, 0, f, :], banks[4 + n % 4][:, :], ACT.Copy, scale=wscale[:, :])\
                        .then_inc(w_hi, 1)

            @block.vector
            def _(dve):
                step = [0]

                def link(ins):
                    step[0] += 1
                    ins.then_inc(dve_done, 1)
                    dve.wait_ge(dve_done, step[0])

                dve.wait_ge(e_in, 16 * len(loads))
                dve.tensor_copy(other[:, :], raw_src[:, :])
                link(dve.tensor_copy(node[:, :], raw_dst[:, :]))
                dve.tensor_tensor(sent, other[:, :], node[:, HERE], ALU.not_equal).then_inc(sent_done, 1)
                dve.tensor_tensor(differs[:, 1:L], node[:, 1:L], node[:, 0:L - 1], ALU.not_equal)
                link(dve.tensor_tensor_reduce(out=scrap[:, :], in0=node[:, HALO - 1:HALO - 1 + W], in1=node[:, HERE],
                                              scale=1.0, scalar=0.0, op0=ALU.subtract, op1=ALU.max,
                                              accum_out=counts[:, 1:2]))
                dve.tensor_scalar(counts[:, 1:2], counts[:, 1:2], 1.0, None, ALU.min)
                dve.tensor_scalar(real[:, :], node[:, HERE], FAR, None, ALU.is_lt)

                for k, arrived in enumerate((wr_in, wl_in)):
                    dve.wait_ge(arrived, 16)
                    ins = dve.tensor_reduce(wmax[:, k:k + 1], raw_w[:, k, :, :], AX.XY, ALU.max,
                                            apply_absolute_value=True)
                link(ins)
                dve.tensor_tensor(wmax[:, 2:3], wmax[:, 0:1], wmax[:, 1:2], ALU.add).then_inc(wmax_ready, 1)

                dve.tensor_tensor(raw_w[:, 0, :, :], raw_w[:, 0, :, :], raw_w[:, 1, :, :], ALU.add)\
                    .then_inc(w_summed, 1)
                dve.wait_ge(positions, 2)
                dve.tensor_tensor(left[:, 0, 1:L], differs[:, 1:L], position[:, 1:L], ALU.mult)
                link(dve.tensor_tensor(right[:, 0, 0:L - 1], differs[:, 1:L], from_end[:, 0:L - 1], ALU.mult))
                dve.wait_ge(wmax_shared, 1)
                link(dve.tensor_scalar(wint[:, 0:1], wmax[:, 3:4].bitcast(i32), 0x7F800000, None, ALU.bitwise_and))
                link(dve.tensor_scalar(wint[:, 0:1], wint[:, 0:1], float(32 << 23), None, ALU.max))
                link(dve.tensor_scalar(wint[:, 1:2], wint[:, 0:1], -1.0, float((254 + 8) << 23), ALU.mult, ALU.add))
                dve.tensor_copy(wscale[:, :], wint[:, 1:2].bitcast(fp32)).then_inc(wscale_ready, 1)
                link(dve.tensor_scalar(wint[:, 0:1], wint[:, 0:1], float(16 << 23), None, ALU.subtract))
                dve.tensor_copy(fold[:, :], wint[:, 0:1].bitcast(fp32))
                for n in range(2 * FC):
                    if n < DOUBLINGS:
                        a, b, reach = n % 2, 1 - n % 2, 1 << n
                        lo, hi = 2 * reach, L - 2 * reach
                        dve.tensor_tensor(left[:, b, lo:L], left[:, a, lo:L], left[:, a, lo - reach:L - reach], ALU.max)
                        link(dve.tensor_tensor(right[:, b, 0:hi], right[:, a, 0:hi], right[:, a, reach:hi + reach],
                                               ALU.max))
                    dve.wait_ge(w_hi, n + 1)
                    wk, f = 1 - n // FC, n % FC
                    dve.scalar_tensor_tensor(weights[:, wk, 1, f, :], banks[4 + n % 4][:, :], wscale[:, :],
                                             weights[:, wk, 0, f, :], ALU.mult, ALU.subtract).then_inc(w_taken, 1)
                assert DOUBLINGS <= 2 * FC
                link(dve.tensor_tensor(degree[:, :], left[:, DOUBLINGS % 2, HERE], right[:, DOUBLINGS % 2, HERE], ALU.add))
                link(dve.tensor_scalar(degree[:, :], degree[:, :], -1.0, float(L + 1), ALU.mult, ALU.add))
                dve.tensor_scalar(skip[:, :], sent, -FAR, FAR, ALU.mult, ALU.add)
                link(dve.tensor_scalar(crowded[:, :], degree[:, :], float(HALO), None, ALU.is_gt))
                link(dve.tensor_tensor_reduce(out=scrap[:, :], in0=crowded[:, :], in1=real[:, :], scale=1.0, scalar=0.0,
                                              op0=ALU.mult, op1=ALU.add, accum_out=counts[:, 2:3]))
                link(dve.tensor_tensor_reduce(out=scrap[:, :], in0=differs[:, HERE], in1=real[:, :], scale=1.0,
                                              scalar=0.0, op0=ALU.mult, op1=ALU.add, accum_out=counts[:, 3:4]))
                dve.wait_ge(prefix_done, 1)
                link(dve.tensor_copy(counts[:, 0:1], prefix[:, (STEPS - 1) % 2, PAD + W - 1:PAD + W]))
                dve.tensor_copy(counts16[:, :], counts[:, :]).then_inc(counted, 1)

                dve.tensor_copy(record[:, 0:W, 2], degree[:, :])
                dve.wait_ge(totalled, 1)
                link(dve.tensor_copy(totals[:, :], banks[0][:, 0:5]))
                link(dve.tensor_scalar(totals[:, 0:1], totals[:, 0:1], -1.0, None, ALU.add))
                link(dve.scalar_tensor_tensor(scrap[:, :], prefix[:, (STEPS - 1) % 2, PAD:PAD + W], totals[:, 0:1], sent,
                                              ALU.add, ALU.mult))
                dve.tensor_tensor(goes_to[:, 0:W], scrap[:, :], skip[:, :], ALU.add)
                link(dve.tensor_scalar(turn_starts[:, :], from0[:, :], float(UNROLL * P), float((LOOP_FROM - 2) * P),
                                       ALU.mult, ALU.add))
                link(dve.tensor_scalar(turn_starts[:, :], turn_starts[:, :], totals[:, 1:2], None, ALU.is_lt))
                link(dve.tensor_reduce(n_turns[:, :], turn_starts[:, :], AX.X, ALU.add))
                dve.tensor_scalar(s.turns[:, :], n_turns[:, :], 1.0, None, ALU.max)
                link(dve.tensor_scalar(bad[:, :], totals[:, 4:5], float(N), None, ALU.not_equal))
                link(dve.tensor_tensor(bad[:, :], bad[:, :], totals[:, 2:3], ALU.add))
                dve.tensor_tensor(s.n_bad[:, :], bad[:, :], totals[:, 3:4], ALU.add)

            @block.tensor
            def _(pe):
                pe.wait_ge(consts, 1)
                pe.wait_ge(wl_in, 16)
                for n in range(2 * FC):
                    if n >= 4:
                        pe.wait_ge(w_taken, n - 3)
                    if n == FC:
                        pe.wait_ge(w_summed, 1)
                    k, f = 1 - n // FC, n % FC
                    for o in range(FC):
                        last = pe.transpose(banks[4 + n % 4][:, o * P:(o + 1) * P],
                                            raw_w[:, k, o, f * P:(f + 1) * P], ident[:, :])
                    last.then_inc(w_turned, 1)
                pe.wait_ge(counted, 1)
                pe.matmul(banks[0][:, 0:1], upper[:, :], counts16[:, 0:1], start=True, stop=True)
                pe.matmul(banks[0][:, 1:5], ones16[:, :], counts16[:, :], start=True, stop=True).then_inc(totalled, 1)


def dense(nc, s, block):
    x, out, D, FC, TILES = s.x, s.out, s.D, s.FC, s.TILES
    weights, bias, fold, banks, SENDS = s.weights, s.bias, s.fold, s.banks, s.SENDS
    def sb(name, shape, dt):
        return s.main.enter_context(nc.sbuf_tensor(name, shape, dt))

    def sem(name):
        return s.main.enter_context(nc.semaphore(name))

    own = sb("own", [P, LONG, D], fp32)
    result = sb("result", [P, MID, D], fp32)
    stats = sb("stats", [P, SHORT, 6], fp32)
    moments = sb("moments", [P, LONG, 2], fp32)
    shifted = sb("shifted", [P, LONG], fp32)
    norm = sb("norm", [P, LONG, 2], fp32)
    power = sb("power", [P, 1], fp32)
    eps = sb("eps", [P, 1], fp32)
    h = sb("h", [P, SHORT, D], fp32)
    turned = sb("turned", [P, SHORT, 2, FC, P], fp16)
    parcels = sb("parcels", [P, 2, SENDS, 4], i32)
    address = sb("address", [P, 2, SENDS], i32)

    h_banks, out_banks = banks[0:2], banks[2:4]

    own_in = [sem(f"own_in{i}") for i in range(LONG)]
    stored = [sem(f"stored{i}") for i in range(MID)]
    records_sent = [sem("records_sent0"), sem("records_sent1")]
    s.edge_in = [sem(f"c_edge_in{i}") for i in range(LONG)]
    parcel_ready = [sem("parcel_ready0"), sem("parcel_ready1")]
    power_set = sem("power_set")
    stats_done, moments_done, shift_done, h_lo_done, base_done, result_done = (
        sem("stats_done"), sem("moments_done"), sem("shift_done"), sem("h_lo_done"), sem("base_done"),
        sem("result_done"))
    shifted_done, rstd_done = sem("shifted_done"), sem("rstd_done")
    h_done, h_hi_done = sem("h_done"), sem("h_hi_done")
    h_turned, out_ready = sem("h_turned"), sem("out_ready")

    TURNS = s.DENSE_TURNS
    s.stored, s.result_done = stored, result_done

    def run(engine, step):
        def at(turn, c):
            def tile(k):
                t = Tile(turn, c + k)
                return t if not t.static or 0 <= t.index < TILES else None
            return tile
        for c in range(-DENSE_AHEAD, LOOP_FROM):
            step(at(0, c))
        with engine.Fori(0, TURNS) as turn:
            for c in range(LOOP_FROM, LOOP_FROM + UNROLL):
                step(at(turn, c))
        for c in range(LOOP_FROM + TURNS * UNROLL, TILES + 1):
            step(at(0, c))

    def is_last(t):
        return t.static and t.index == TILES - 1

    @block.sync
    def _(sp):
        def step(at):
            if t := at(-1):
                after(sp, result_done, t)
                if is_last(t):
                    sp.dma_start(out[s.N - s.LAST_NEW:s.N, :], result[P - s.LAST_NEW:P, t.slot(MID), :])\
                        .then_inc(stored[t.slot(MID)], 16)
                else:
                    sp.dma_start(out[bass.ds(t.index * P, P), :], result[:, t.slot(MID), :])\
                        .then_inc(stored[t.slot(MID)], 16)
            if t := at(5):
                after(sp, base_done, t, LONG)
                first = s.LAST_BASE if is_last(t) else t.index * P
                sp.dma_start(own[:, t.slot(LONG), :], x[bass.ds(first, P), :])\
                    .then_inc(own_in[t.slot(LONG)], 16)
            if (t := at(4)) and is_last(t):
                for half in range(2):
                    sp.wait_ge(records_sent[half], 16 * SENDS * (TURNS + 1))
                for unit in range(LONG):
                    sp.dma_start(s.edge[:, unit, :], s.records[unit * P:(unit + 1) * P, :])\
                        .then_inc(s.edge_in[unit], 16)

        run(sp, step)

    @block.gpsimd
    def _(pool):
        pool.memset(power[:, :], -0.5).then_inc(power_set, 1)
        pool.memset(eps[:, :], EPS).then_inc(power_set, 1)
        pool.wait_ge(power_set, 2)

        last_record = pool.alloc_register("last_record")
        pool.reg_mov(last_record, s.UNITS * P - 1)

        def send(half, j):
            pool.indirect_dma_start(
                out=s.records[:, :], out_offset=bass.IndirectOffsetOnAxis(ap=address[:, half, j:j + 1], axis=0),
                in_=parcels[:, half, j, :], in_offset=None, bounds_check=last_record, oob_is_err=False)\
                .then_inc(records_sent[half], 16)

        def step(at):
            if parcel := parcel_of(at):
                turn, half, third = parcel
                if third == 0:
                    column = (turn + 1) * (2 * SENDS) + half * SENDS
                    if not isinstance(turn, int):
                        pool.wait_ge(records_sent[half], (turn + 1) * (16 * SENDS))
                    pool.tensor_copy(parcels[:, half, :, :], s.record[:, bass.ds(column, SENDS), :])\
                        .then_inc(parcel_ready[half], 1)
                    pool.tensor_copy(address[:, half, :], s.goes_to[:, bass.ds(column, SENDS)])\
                        .then_inc(parcel_ready[half], 1)
                    pool.wait_ge(parcel_ready[half], (turn + 2) * 2)
            if t := at(2):
                b = t.slot(LONG)
                after(pool, moments_done, t)
                pool.tensor_tensor(shifted[:, b:b + 1], moments[:, b, 1:2], eps[:, :], ALU.add)\
                    .then_inc(shifted_done, 1)
                after(pool, shifted_done, t)
                pool.tensor_tensor(norm[:, b, 0:1], shifted[:, b:b + 1], power[:, :], ALU.pow)\
                    .then_inc(rstd_done, 1)
            if parcel:
                for j in range(third * SENDS // 3, (third + 1) * SENDS // 3):
                    send(half, j)

        def parcel_of(at):
            t = at(2)
            if t is None or t.static and t.index - 2 >= LOOP_FROM:
                return None
            turn, sixth = (-1, t.c - 2 - LOOP_FROM + UNROLL) if t.static else (t.turn, t.c - 2 - LOOP_FROM)
            return (turn, *divmod(sixth, UNROLL // 2))

        run(pool, step)

    @block.scalar
    def _(act):
        def step(at):
            if t := at(1):
                after(act, h_turned, t)
                after(act, out_ready, t, SHORT)
                act.activation(turned[:, t.slot(SHORT), 0], h_banks[t.slot(2)][:, :], ACT.Copy, scale=SCALE)\
                    .then_inc(h_hi_done, 1)
            if t := at(2):
                b, d = t.slot(LONG), t.slot(SHORT)
                after(act, shift_done, t)
                after(act, h_turned, t, SHORT)
                act.activation(h[:, d, :], own[:, b, :], ACT.Relu, bias=norm[:, b, 1:2],
                               scale=norm[:, b, 0:1]).then_inc(h_done, 1)

        run(act, step)

    @block.vector
    def _(dve):
        def step(at):
            if t := at(-1):
                after(dve, base_done, t)
                after(dve, out_ready, t)
                dve.scalar_tensor_tensor(result[:, t.slot(MID), :], out_banks[t.slot(2)][:, :], fold[:, :],
                                         result[:, t.slot(MID), :], ALU.mult, ALU.add)\
                    .then_inc(result_done, 1)
            if t := at(0):
                d = t.slot(SHORT)
                after(dve, h_hi_done, t)
                dve.scalar_tensor_tensor(turned[:, d, 1], h_banks[t.slot(2)][:, :], SCALE, turned[:, d, 0],
                                         ALU.mult, ALU.subtract).then_inc(h_lo_done, 1)
            if t := at(3):
                dve.wait_ge(own_in[t.slot(LONG)], 16 * t.nth(LONG))
                dve.bn_stats(stats[:, t.slot(SHORT), :], own[:, t.slot(LONG), :]).then_inc(stats_done, 1)
            if t := at(2):
                b = t.slot(LONG)
                after(dve, rstd_done, t)
                dve.scalar_tensor_tensor(norm[:, b, 1:2], moments[:, b, 0:1], -1.0, norm[:, b, 0:1],
                                         ALU.mult, ALU.mult).then_inc(shift_done, 1)
            if t := at(0):
                if at(3):
                    after(dve, stats_done, at(3))
                if not t.static or t.index >= MID:
                    dve.wait_ge(stored[t.slot(MID)], 16 * (t.nth(MID) - 1))
                dve.tensor_tensor(result[:, t.slot(MID), :], bias[:, :], own[:, t.slot(LONG), :], ALU.add)\
                    .then_inc(base_done, 1)
            if t := at(3):
                if t.static:
                    after(dve, stats_done, t)
                dve.bn_aggr(moments[:, t.slot(LONG), :], stats[:, t.slot(SHORT), :]).then_inc(moments_done, 1)

        run(dve, step)

    @block.tensor
    def _(pe):
        def step(at):
            if t := at(0):
                d = t.slot(SHORT)
                after(pe, h_hi_done, t)
                after(pe, result_done, t, 2)
                for f in range(FC):
                    for part in range(2):
                        pe.matmul(out_banks[t.slot(2)][:, :], turned[:, d, 0, f, :], weights[:, 0, part, f, :],
                                  start=(f == part == 0), stop=False)
            if t := at(1):
                after(pe, h_done, t)
                after(pe, h_lo_done, t, 2)
                for f in range(FC):
                    last = pe.transpose(h_banks[t.slot(2)][:, f * P:(f + 1) * P],
                                        h[:, t.slot(SHORT), f * P:(f + 1) * P], s.ident[:, :])
                last.then_inc(h_turned, 1)
            if t := at(0):
                after(pe, h_lo_done, t)
                for f in range(FC):
                    last = pe.matmul(out_banks[t.slot(2)][:, :], turned[:, d, 1, f, :], weights[:, 0, 0, f, :],
                                     start=False, stop=(f == FC - 1))
                last.then_inc(out_ready, 1)

        run(pe, step)


def correct(nc, s, block):
    x, out, D, FC = s.x, s.out, s.D, s.FC
    weights, fold, banks = s.weights, s.fold, s.banks
    def sb(name, shape, dt):
        return s.main.enter_context(nc.sbuf_tensor(name, shape, dt))

    def sem(name):
        return s.main.enter_context(nc.semaphore(name))

    edge, edge_in, rows = s.edge, s.edge_in, s.rows
    edge_f = sb("c_edge_f", [P, LONG, 2], fp32)
    share = sb("c_share", [P, LONG, 1], fp32)
    same = sb("c_same", [P, LONG, P], fp32)
    scrap = sb("c_scrap", [P, LONG, P], fp32)
    before = sb("c_before", [P, LONG, 1], fp32)
    target = sb("c_target", [P, LONG, 1], i32)
    stats = sb("c_stats", [P, SHORT, 2, 6], fp32)
    moments = sb("c_moments", [P, LONG, 2, 2], fp32)
    shifted = sb("c_shifted", [P, LONG, 2], fp32)
    norm = sb("c_norm", [P, LONG, 2, 2], fp32)
    norm_in = sb("c_norm_in", [P, LONG, 2, 2], fp32)
    power = sb("c_power", [P, 2, 2], fp32)
    eps = sb("c_eps", [P, 2], fp32)
    h = sb("c_h", [P, SHORT, 2, D], fp32)
    diff = sb("c_diff", [P, MID, D], fp32)
    turned = sb("c_turned", [P, SHORT, 2, FC, P], fp16)
    addend = sb("c_addend", [P, MID, D], fp32)

    dst_banks, sum_banks, out_banks = banks[4:6], banks[6:8], banks[2:4]

    rows_in = [sem(f"c_rows_in{i}") for i in range(LONG)]
    added, power_set = sem("c_added"), sem("c_power_set")
    drained = sem("c_drained")
    edge_f_done, share_done, same_done, before_done, target_done = (
        sem("c_edge_f"), sem("c_share_done"), sem("c_same_done"), sem("c_before_done"), sem("c_target_done"))
    stats_done, moments_done, shift_done, norm_in_done = (
        sem("c_stats_done"), sem("c_moments_done"), sem("c_shift_done"), sem("c_norm_in_done"))
    diff_done, sum_lo_done = sem("c_diff_done"), sem("c_sum_lo_done")
    shifted_done, rstd_done = sem("c_shifted_done"), sem("c_rstd_done")
    h_done, sum_hi_done, addend_done = sem("c_h_done"), sem("c_sum_hi_done"), sem("c_addend_done")
    dst_spread, summed, out_ready = sem("c_dst_spread"), sem("c_summed"), sem("c_out_ready")

    def run(engine, step):
        def at(turn, c):
            def unit(k):
                t = Tile(turn, c + k)
                return t if not t.static or t.index >= 0 else None
            return unit
        for c in range(-UNITS_AHEAD, LOOP_FROM):
            step(at(0, c))
        turns = engine.snap(engine.value_load(s.turns[0:1, 0:1], min_val=1, max_val=s.MAX_TURNS),
                            min_val=1, max_val=s.MAX_TURNS)
        with engine.Fori(0, turns) as turn:
            for c in range(LOOP_FROM, LOOP_FROM + UNROLL):
                step(at(turn, c))
        return at(turns, LOOP_FROM - 1)

    @block.sync
    def _(sp):
        def step(at):
            if (t := at(9)) and not (t.static and t.index < LONG):
                after(sp, stats_done, t, LONG)
                sp.dma_start(edge[:, t.slot(LONG), :], s.records[bass.ds(t.index * P, P), :])\
                    .then_inc(edge_in[t.slot(LONG)], 16)

        run(sp, step)

    @block.gpsimd
    def _(pool):
        pool.memset(power[:, :, :], -0.5).then_inc(power_set, 1)
        pool.memset(eps[:, :], EPS).then_inc(power_set, 1)
        pool.wait_ge(power_set, 2)

        last_row = pool.alloc_register("c_last_row")
        pool.reg_mov(last_row, s.N - 1)
        steps_over = pool.alloc_register("c_steps_over")
        pool.reg_mov(steps_over, 0)

        def step(at):
            g, a = at(8), at(-2)
            if g:
                pool.wait_ge(edge_in[g.slot(LONG)], 16 * g.nth(LONG))
                after(pool, h_done, g, LONG)
            if a:
                if a.static and a.index == 0:
                    for n in range(s.TILES - MID, s.TILES):
                        tile = Tile(0, n)
                        pool.wait_ge(s.stored[tile.slot(MID)], 16 * tile.nth(MID))
                after(pool, addend_done, a)
                after(pool, target_done, a)
                after(pool, added, a, 1, by=16)
            if t := at(5):
                after(pool, moments_done, t)
                pool.tensor_tensor(shifted[:, t.slot(LONG), :], moments[:, t.slot(LONG), :, 1], eps[:, :],
                                   ALU.add).then_inc(shifted_done, 1)
            if a:
                pool.indirect_dma_start(
                    out=out[:, :], out_offset=bass.IndirectOffsetOnAxis(ap=target[:, a.slot(LONG), :], axis=0),
                    in_=addend[:, a.slot(MID), :], in_offset=None, bounds_check=last_row, oob_is_err=False,
                    compute_op=ALU.add).then_inc(added, 16)
            if (t := at(4)) and t.c % 2 == 0:
                pair = slice(t.slot(LONG), t.slot(LONG) + 2)
                after(pool, shifted_done, at(5))
                pool.tensor_tensor(norm[:, pair, 0, :], shifted[:, pair, :], power[:, :, :], ALU.pow)\
                    .then_inc(rstd_done, 2)
            if g:
                for k in range(2):
                    pool.indirect_dma_start(
                        out=rows[:, g.slot(LONG), k, :], out_offset=None, in_=x[:, :],
                        in_offset=bass.IndirectOffsetOnAxis(ap=edge[:, g.slot(LONG), k:k + 1], axis=0),
                        bounds_check=last_row, oob_is_err=False).then_inc(rows_in[g.slot(LONG)], 16)

        at = run(pool, step)
        after(pool, added, at(-2), by=16)
        pool.reg_add(steps_over, steps_over, 1)
        pool.wait_ge(rows_in[at(8).slot(LONG)], 32 * at(8).nth(LONG))
        pool.reg_add(steps_over, steps_over, 1)
        pool.wait_ge(edge_in[at(9).slot(LONG)], 16 * at(9).nth(LONG))
        pool.reg_add(steps_over, steps_over, 1)

    @block.scalar
    def _(act):
        def step(at):
            if t := at(-1):
                after(act, out_ready, t)
                after(act, added, t, MID, by=16)
                act.activation(addend[:, t.slot(MID), :], out_banks[t.slot(2)][:, :], ACT.Copy,
                               scale=fold[:, :]).then_inc(addend_done, 1)
            if t := at(1):
                after(act, summed, t)
                after(act, out_ready, t, SHORT)
                act.activation(turned[:, t.slot(SHORT), 0], sum_banks[t.slot(2)][:, :], ACT.Copy)\
                    .then_inc(sum_hi_done, 1)
            if t := at(3):
                b, d = t.slot(LONG), t.slot(SHORT)
                after(act, norm_in_done, t)
                after(act, diff_done, t, SHORT)
                for k in range(2):
                    last = act.activation(h[:, d, k, :], rows[:, b, k, :], ACT.Relu,
                                          bias=norm_in[:, b, 1, k:k + 1], scale=norm_in[:, b, 0, k:k + 1])
                last.then_inc(h_done, 1)

        run(act, step)

    @block.vector
    def _(dve):
        dve.wait_ge(power_set, 2)

        def step(at):
            if t := at(0):
                d = t.slot(SHORT)
                after(dve, sum_hi_done, t)
                dve.tensor_tensor(turned[:, d, 1], sum_banks[t.slot(2)][:, :], turned[:, d, 0],
                                  ALU.subtract).then_inc(sum_lo_done, 1)
            if t := at(3):
                b3 = t.slot(LONG)
                after(dve, rstd_done, t)
                dve.scalar_tensor_tensor(norm[:, b3, 1, :], moments[:, b3, :, 0], -1.0, norm[:, b3, 0, :],
                                         ALU.mult, ALU.mult).then_inc(shift_done, 1)
            if t := at(4):
                b4 = t.slot(LONG)
                after(dve, dst_spread, t)
                after(dve, summed, t, LONG)
                dve.tensor_scalar(same[:, b4, :], dst_banks[t.slot(2)][:, 0:P], edge_f[:, b4, 0:1], None,
                                  ALU.is_equal).then_inc(same_done, 1)
            if t := at(3):
                after(dve, shift_done, t)
                after(dve, share_done, t)
                dve.tensor_scalar(norm_in[:, b3, :, :], norm[:, b3, :, :], share[:, b3, :], SCALE,
                                  ALU.mult, ALU.mult).then_inc(norm_in_done, 1)
            if t := at(2):
                after(dve, h_done, t)
                after(dve, summed, t, MID)
                dve.tensor_tensor(diff[:, t.slot(MID), :], h[:, t.slot(SHORT), 0, :], h[:, t.slot(SHORT), 1, :],
                                  ALU.subtract).then_inc(diff_done, 1)
            if t := at(6):
                dve.wait_ge(edge_in[t.slot(LONG)], 16 * t.nth(LONG))
                after(dve, target_done, t, LONG)
                dve.tensor_copy(edge_f[:, t.slot(LONG), :], edge[:, t.slot(LONG), 1:3]).then_inc(edge_f_done, 1)
            if t := at(4):
                after(dve, same_done, t)
                dve.tensor_tensor_reduce(out=scrap[:, b4, :], in0=same[:, b4, :], in1=s.lower[:, :], scale=1.0,
                                         scalar=0.0, op0=ALU.mult, op1=ALU.add,
                                         accum_out=before[:, b4, :]).then_inc(before_done, 1)
            if t := at(6):
                b6, d6 = t.slot(LONG), t.slot(SHORT)
                dve.wait_ge(rows_in[b6], 32 * t.nth(LONG))
                dve.bn_stats(stats[:, d6, 0, :], rows[:, b6, 0, :])
                dve.bn_stats(stats[:, d6, 1, :], rows[:, b6, 1, :]).then_inc(stats_done, 1)
            if t := at(5):
                after(dve, edge_f_done, t)
                dve.reciprocal(share[:, t.slot(LONG), :], edge_f[:, t.slot(LONG), 1:2]).then_inc(share_done, 1)
            if t := at(2):
                after(dve, before_done, t)
                after(dve, added, t, LONG, by=16)
                after(dve, stats_done, at(6))
                dve.scalar_tensor_tensor(target[:, t.slot(LONG), :], before[:, t.slot(LONG), :], FAR,
                                         edge_f[:, t.slot(LONG), 0:1], ALU.mult, ALU.add)\
                    .then_inc(target_done, 1)
            if t := at(6):
                if t.static:
                    after(dve, stats_done, t)
                dve.bn_aggr(moments[:, b6, 0, :], stats[:, d6, 0, :])
                dve.bn_aggr(moments[:, b6, 1, :], stats[:, d6, 1, :]).then_inc(moments_done, 1)

        run(dve, step)

    @block.tensor
    def _(pe):
        def step(at):
            if t := at(1):
                b, d = t.slot(LONG), t.slot(SHORT)
                after(pe, same_done, t)
                after(pe, diff_done, t)
                after(pe, sum_lo_done, t, 2)
                for f in range(FC):
                    c = slice(f * P, (f + 1) * P)
                    last = pe.matmul(sum_banks[t.slot(2)][:, c], diff[:, t.slot(MID), c], same[:, b, :],
                                     start=True, stop=True)
                last.then_inc(summed, 1)
            if t := at(0):
                d = t.slot(SHORT)
                if t.static and t.index == 0:
                    pe.wait_ge(s.result_done, s.TILES)
                after(pe, sum_hi_done, t)
                after(pe, addend_done, t, 2)
                for f in range(FC):
                    for part in range(2):
                        pe.matmul(out_banks[t.slot(2)][:, :], turned[:, d, 0, f, :], weights[:, 1, part, f, :],
                                  start=(f == part == 0), stop=False)
            if t := at(5):
                b = t.slot(LONG)
                after(pe, edge_f_done, t)
                after(pe, same_done, t, 2)
                pe.matmul(dst_banks[t.slot(2)][:, 0:P], edge_f[:, b, 0:1].broadcast_to([P, P]), s.ident[:, :],
                          start=True, stop=True).then_inc(dst_spread, 1)
            if t := at(0):
                after(pe, sum_lo_done, t)
                for f in range(FC):
                    last = pe.matmul(out_banks[t.slot(2)][:, :], turned[:, d, 1, f, :], weights[:, 1, 0, f, :],
                                     start=False, stop=(f == FC - 1))
                last.then_inc(out_ready, 1)

        run(pe, step)


def ranges(nc, s):
    E, EG, COLS, NSUB, ROW, TG, TCOLS, LAST_BASE = s.E, s.EG, s.COLS, s.NSUB, s.ROW, s.TG, s.TCOLS, s.LAST_BASE
    ident, ones, table, src_of, tinfo, banks = s.ident, s.ones, s.table, s.src_of, s.tinfo, s.banks
    with ExitStack() as ctx:
        def sb(name, shape, dt):
            return ctx.enter_context(nc.sbuf_tensor(name, shape, dt))

        def sem(name):
            return ctx.enter_context(nc.semaphore(name))

        raw_dst = sb("r_dst", [P, EG, P], i32)
        raw_src = sb("r_src", [P, EG, P], i32)
        cut = sb("r_cut", [P, 2, EG, P], i32)
        edge = sb("r_edge", [P, 4, EG, P], fp32)
        subs = sb("r_subs", [P, 2, EG * NSUB], fp32)
        diag = sb("r_diag", [P, 2, 4, P], fp32)
        rows = sb("r_rows", [P, 2, ROW], fp32)
        end_id = sb("r_end_id", [P, ROW], fp32)
        rev_id = sb("r_rev_id", [P, ROW], fp32)
        meet = sb("r_meet", [P, ROW], fp32)
        scrap = sb("r_scrap", [P, ROW], fp32)
        base_col = sb("r_base_col", [P, TG, 2], fp32)
        found = sb("r_found", [P, TG, 2], fp32)
        info = sb("r_info", [P, 3, TG], fp32)

        e_filled, e_in, consts, dve_done = sem("r_e_filled"), sem("r_e_in"), sem("r_consts"), sem("r_dve_done")
        edge_ready, edge_turned, edge_taken = sem("r_edge_ready"), sem("r_edge_turned"), sem("r_edge_taken")
        diag_ready, row_ready, row_taken = sem("r_diag_ready"), sem("r_row_ready"), sem("r_row_taken")

        full, rest = E // P, E % P
        edge_loads = []
        for raw, flat in ((raw_dst, s.dst), (raw_src, s.src)):
            for g in range(EG):
                n = min(P, full - g * P)
                if n > 0:
                    edge_loads.append((raw[0:n, g, :], flat[g * P * P:(g * P + n) * P].rearrange("(q e) -> q e", e=P)))
            if rest:
                q = full % P
                edge_loads.append((raw[q:q + 1, full // P, 0:rest], flat[full * P:E].rearrange("(a e) -> a e", a=1)))

        def needed(engine):
            return engine.If(engine.value_load(s.n_bad[0:1, 0:1], min_val=0, max_val=4 * E) > 0)

        with nc.Block(name="ranges") as block:
            @block.sync
            def _(sp):
                with needed(sp):
                    sp.wait_ge(e_filled, 2)
                    for to, frm in edge_loads:
                        sp.dma_start(to, frm).then_inc(e_in, 16)

            @block.gpsimd
            def _(pool):
                with needed(pool):
                    pool.memset(raw_dst[:, :, :], int(FAR)).then_inc(e_filled, 1)
                    pool.memset(raw_src[:, :, :], 0).then_inc(e_filled, 1)
                    pool.iota(base_col[:, :, 0], pattern=[[P * P, TG]], base=0, channel_multiplier=P,
                              allow_small_or_imprecise_dtypes=True).then_inc(consts, 1)
                    pool.iota(end_id[:, :], pattern=[[P, EG], [0, NSUB], [1, P]], base=1, channel_multiplier=0,
                              allow_small_or_imprecise_dtypes=True).then_inc(consts, 1)

            @block.vector
            def _(dve):
                step = [0]

                def link(ins):
                    step[0] += 1
                    ins.then_inc(dve_done, 1)
                    dve.wait_ge(dve_done, step[0])

                def table_of_edges():
                    dve.wait_ge(consts, 2)
                    dve.wait_ge(e_in, 16 * len(edge_loads))
                    dve.tensor_copy(edge[:, 0, :, :], raw_dst[:, :, :])
                    link(dve.tensor_copy(edge[:, 2, :, :], raw_src[:, :, :]))
                    link(dve.tensor_tensor(edge[:, 1, :, :], edge[:, 0, :, :], edge[:, 2, :, :], ALU.not_equal))
                    dve.tensor_scalar(cut[:, 0, :, :], raw_src[:, :, :], 8, None, ALU.logical_shift_right)
                    link(dve.tensor_scalar(cut[:, 1, :, :], raw_src[:, :, :], 255, None, ALU.bitwise_and))
                    dve.tensor_scalar(edge[:, 2, :, :], cut[:, 0, :, :], -512.0, None, ALU.add)
                    dve.tensor_copy(edge[:, 3, :, :], cut[:, 1, :, :]).then_inc(edge_ready, 1)
                    for g in range(EG):
                        dve.wait_ge(edge_turned, g + 1)
                        dve.tensor_copy(table[:, g * P:(g + 1) * P, 0:4],
                                        banks[2 + g % 2].rearrange("p (k q) -> p q k", k=4)).then_inc(edge_taken, 1)
                    dve.wait_ge(edge_taken, EG)
                    link(dve.tensor_scalar(scrap[:, 0:COLS], table[:, 0:COLS, 2], 512.0, 256.0, ALU.add, ALU.mult))
                    dve.tensor_tensor(src_of[:, :], scrap[:, 0:COLS], table[:, 0:COLS, 3], ALU.add)

                turns = [0]

                def row_turn(columns, take):
                    n = turns[0]
                    if n >= 2:
                        dve.wait_ge(row_ready, n - 1)
                    for k, column in enumerate(columns):
                        ins = dve.tensor_scalar(diag[:, n % 2, k, :], ident[:, :], column, None, ALU.mult)
                    ins.then_inc(diag_ready, 1)
                    dve.wait_ge(row_ready, n + 1)
                    take(banks[n % 2]).then_inc(row_taken, 1)
                    turns[0] += 1

                with needed(dve):
                    table_of_edges()
                    by_sub = edge[:, 0, :, :].rearrange("p g (s e) -> p (g s) e", e=SUB)
                    dve.tensor_reduce(subs[:, 0, :], by_sub, AX.X, ALU.min)
                    link(dve.tensor_reduce(subs[:, 1, :], by_sub, AX.X, ALU.max))
                    link(dve.tensor_scalar(base_col[:, :, 0], base_col[:, :, 0], float(LAST_BASE), None, ALU.min))
                    dve.tensor_scalar(base_col[:, :, 1], base_col[:, :, 0], float(P), None, ALU.add)
                    link(dve.tensor_scalar(rev_id[:, :], end_id[:, :], -1.0, float(COLS + 1), ALU.mult, ALU.add))
                    flat_subs, flat_rows = (subs[:, :, :].rearrange("p k c -> p (k c)"),
                                            rows[:, :, :].rearrange("p k c -> p (k c)"))
                    for c in range(0, 2 * EG * NSUB, 4):
                        w = min(4, 2 * EG * NSUB - c)
                        row_turn([flat_subs[:, c + i:c + i + 1] for i in range(w)],
                                 lambda bank: dve.tensor_copy(flat_rows[:, c * P:(c + w) * P], bank[:, 0:w * P]))
                    link(dve.memset(found[:, :, :], 0.0))
                    for g in range(TG):
                        link(dve.tensor_scalar(meet[:, :], rows[:, 1, :], base_col[:, g, 0:1], None, ALU.is_ge))
                        link(dve.scalar_tensor_tensor(meet[:, :], rows[:, 0, :], base_col[:, g, 1:2], meet[:, :],
                                                      ALU.is_lt, ALU.mult))
                        for k, weight in enumerate((rev_id[:, :], end_id[:, :])):
                            link(dve.tensor_tensor_reduce(out=scrap[:, :], in0=meet[:, :], in1=weight, scale=1.0,
                                                          scalar=0.0, op0=ALU.mult, op1=ALU.max,
                                                          accum_out=found[:, g, k:k + 1]))
                    link(dve.tensor_scalar(info[:, 0, :], found[:, :, 0], -1.0, float(COLS), ALU.mult, ALU.add))
                    link(dve.tensor_scalar(info[:, 0, :], info[:, 0, :], float(COLS - 1), None, ALU.min))
                    link(dve.scalar_tensor_tensor(info[:, 1, :], info[:, 0, :], 1.0, found[:, :, 1], ALU.add, ALU.max))
                    link(dve.tensor_copy(info[:, 2, :], base_col[:, :, 0]))
                    for k in range(3):
                        for c in range(0, TG, 4):
                            w = min(4, TG - c)
                            row_turn([info[:, k, c + i:c + i + 1] for i in range(w)],
                                     lambda bank: dve.tensor_copy(tinfo[:, k, c * P:(c + w) * P], bank[:, 0:w * P]))

            @block.tensor
            def _(pe):
                with needed(pe):
                    pe.wait_ge(edge_ready, 1)
                    for g in range(EG):
                        if g >= 2:
                            pe.wait_ge(edge_taken, g - 1)
                        for k in range(4):
                            last = pe.transpose(banks[2 + g % 2][:, k * P:(k + 1) * P], edge[:, k, g, :], ident[:, :])
                        last.then_inc(edge_turned, 1)
                    widths = ([min(4, 2 * EG * NSUB - c) for c in range(0, 2 * EG * NSUB, 4)]
                              + 3 * [min(4, TG - c) for c in range(0, TG, 4)])
                    for n, width in enumerate(widths):
                        pe.wait_ge(diag_ready, n + 1)
                        if n >= 2:
                            pe.wait_ge(row_taken, n - 1)
                        pe.matmul(banks[n % 2][:, 0:width * P], ones[:, :], diag[:, n % 2, 0:width, :],
                                  start=True, stop=True).then_inc(row_ready, 1)


def general(nc, s):
    x, out, D, FC, TILES = s.x, s.out, s.D, s.FC, s.TILES
    ident, ones16, from0 = s.ident, s.ones16, s.from0
    weights, fold, table, tinfo, banks = s.weights, s.fold, s.table, s.tinfo, s.banks
    with ExitStack() as ctx:
        def sb(name, shape, dt):
            return ctx.enter_context(nc.sbuf_tensor(name, shape, dt))

        def sem(name):
            return ctx.enter_context(nc.semaphore(name))

        own = sb("g_own", [P, D], fp32)
        far = sb("g_far", [P, D], fp32)
        result = sb("g_result", [P, D], fp32)
        row_id = sb("g_row_id", [P, 1], i32)
        base = sb("g_base", [P, 1], fp32)
        local = sb("g_local", [P, 1], fp32)
        to_node = sb("g_to_node", [P, P], fp16)
        zeros = sb("g_zeros", [P, D], fp16)
        stats = sb("g_stats", [P, 6], fp32)
        moments = sb("g_moments", [P, 2], fp32)
        shifted = sb("g_shifted", [P, 1], fp32)
        power = sb("g_power", [P, 1], fp32)
        eps = sb("g_eps", [P, 1], fp32)
        rstd = sb("g_rstd", [P, 1], fp32)
        shift = sb("g_shift", [P, 1], fp32)
        h = sb("g_h", [P, D], fp32)
        h_hi = sb("g_h_hi", [P, D], fp16)
        h_lo = sb("g_h_lo", [P, D], fp16)
        inverse = sb("g_inverse", [P, P], fp32)
        mean = sb("g_mean", [P, FC, P], fp32)
        has_edge = sb("g_has_edge", [P, 1], fp32)
        turned = sb("g_turned", [P, 2, 2, FC, P], fp16)
        h_bank, mean_bank, degree_bank, out_bank = banks[0:4]

        own_in, far_in, stored = sem("g_own_in"), sem("g_far_in"), sem("g_stored")
        pool_own, dve_own = sem("g_pool_own"), sem("g_dve_own")
        set_up = sem("g_set_up")
        moments_done, rstd_done, item_ready, item_used = (
            sem("g_moments"), sem("g_rstd"), sem("g_item_ready"), sem("g_item_used"))
        mean_split, out_ready, result_done = sem("g_mean_split"), sem("g_out_ready"), sem("g_result_done")

        class Count:

            def __init__(self, engine, name):
                self.engine, self.reg = engine, engine.alloc_register(name)
                engine.reg_mov(self.reg, 0)

            def value(self):
                return self.engine.snap(self.reg)

            def add(self):
                self.engine.reg_add(self.reg, self.reg, 1)

        def tile_by_tile(engine, own_part, chunk_part, tile_part):
            with engine.If(engine.value_load(s.n_bad[0:1, 0:1], min_val=0, max_val=4 * s.E) > 0):
                with engine.Fori(0, TILES) as t:
                    own_part(t)
                    first = engine.value_load(tinfo[0:1, 0, bass.ds(t, 1)], min_val=0, max_val=s.COLS)
                    end = engine.value_load(tinfo[0:1, 1, bass.ds(t, 1)], min_val=0, max_val=s.COLS)
                    with engine.Fori(first, end) as chunk:
                        chunk_part(engine.snap(chunk, min_val=0, max_val=s.COLS - 1))
                    tile_part(t)

        with nc.Block(name="general") as block:
            @block.gpsimd
            def _(pool):
                items, tiles, chunks, own_steps = (Count(pool, "pool_items"), Count(pool, "pool_tiles"),
                                                   Count(pool, "pool_chunks"), Count(pool, "pool_steps"))
                pool.memset(power[:, :], -0.5).then_inc(set_up, 1)
                pool.memset(eps[:, :], EPS).then_inc(set_up, 1)
                pool.memset(zeros[:, :], 0.0).then_inc(set_up, 1)
                pool.wait_ge(set_up, 3)

                last_row = pool.alloc_register("g_last_row")
                pool.reg_mov(last_row, s.N - 1)

                def own_step(ins):
                    ins.then_inc(pool_own, 1)
                    pool.wait_ge(pool_own, own_steps.value() + 1)
                    own_steps.add()

                def normalise():
                    pool.wait_ge(moments_done, items.value() + 1)
                    own_step(pool.tensor_tensor(shifted[:, :], moments[:, 1:2], eps[:, :], ALU.add))
                    pool.tensor_tensor(rstd[:, :], shifted[:, :], power[:, :], ALU.pow).then_inc(rstd_done, 1)
                    pool.wait_ge(item_used, items.value() + 1)
                    items.add()

                def own_part(t):
                    first = pool.value_load(tinfo[0:1, 2, bass.ds(t, 1)], min_val=0, max_val=s.LAST_BASE)
                    pool.dma_start(own[:, :], x[bass.ds(first, P), :]).then_inc(own_in, 16)
                    normalise()

                def chunk_part(chunk):
                    own_step(pool.tensor_copy(row_id[:, :], s.src_of[:, bass.ds(chunk, 1)]))
                    pool.indirect_dma_start(
                        out=far[:, :], out_offset=None, in_=x[:, :],
                        in_offset=bass.IndirectOffsetOnAxis(ap=row_id[:, :], axis=0),
                        bounds_check=last_row, oob_is_err=False).then_inc(far_in, 16)
                    normalise()

                def tile_part(t):
                    pool.wait_ge(result_done, tiles.value() + 1)
                    tiles.add()
                    first = pool.value_load(tinfo[0:1, 2, bass.ds(t, 1)], min_val=0, max_val=s.LAST_BASE)
                    pool.dma_start(out[bass.ds(first, P), :], result[:, :]).then_inc(stored, 16)
                    pool.wait_ge(stored, tiles.value() * 16)

                tile_by_tile(pool, own_part, chunk_part, tile_part)

            @block.vector
            def _(dve):
                items, tiles, chunks, own_steps = (Count(dve, "dve_items"), Count(dve, "dve_tiles"),
                                                   Count(dve, "dve_chunks"), Count(dve, "dve_steps"))

                def own_step(ins):
                    ins.then_inc(dve_own, 1)
                    own_steps.add()
                    dve.wait_ge(dve_own, own_steps.value())

                def normalise(rows, meanwhile):
                    own_step(dve.bn_stats(stats[:, :], rows))
                    meanwhile()
                    dve.bn_aggr(moments[:, :], stats[:, :]).then_inc(moments_done, 1)
                    dve.wait_ge(rstd_done, items.value() + 1)
                    own_step(dve.scalar_tensor_tensor(shift[:, :], moments[:, 0:1], -1.0, rstd[:, :],
                                                      ALU.mult, ALU.mult))
                    own_step(dve.tensor_scalar(h[:, :], rows, rstd[:, :], shift[:, :], ALU.mult, ALU.add))

                def own_part(t):
                    dve.wait_ge(own_in, tiles.value() * 16 + 16)
                    normalise(own[:, :], lambda: dve.tensor_copy(base[:, :], tinfo[:, 2, bass.ds(t, 1)]))
                    dve.tensor_scalar(h[:, :], h[:, :], 0.0, None, ALU.max).then_inc(item_ready, 1)
                    dve.wait_ge(item_used, items.value() + 1)
                    own_step(dve.tensor_scalar(turned[:, 0, 0], h_bank[:, :], SCALE, None, ALU.mult))
                    own_step(dve.scalar_tensor_tensor(turned[:, 0, 1], h_bank[:, :], SCALE, turned[:, 0, 0],
                                                      ALU.mult, ALU.subtract))
                    items.add()

                def chunk_part(chunk):
                    dve.wait_ge(far_in, chunks.value() * 16 + 16)

                    def nodes():
                        own_step(dve.tensor_scalar(local[:, :], table[:, bass.ds(chunk, 1), 0], base[:, :], None,
                                                   ALU.subtract))
                        dve.tensor_scalar(to_node[:, :], from0[:, :], local[:, :], None, ALU.is_equal)

                    normalise(far[:, :], nodes)
                    own_step(dve.tensor_scalar(h[:, :], h[:, :], 0.0, SCALE, ALU.max, ALU.mult))
                    own_step(dve.tensor_copy(h_hi[:, :], h[:, :]))
                    dve.tensor_tensor(h_lo[:, :], h[:, :], h_hi[:, :], ALU.subtract).then_inc(item_ready, 1)
                    dve.wait_ge(item_used, items.value() + 1)
                    items.add()
                    chunks.add()

                def tile_part(t):
                    own_step(dve.tensor_scalar(inverse[:, :], degree_bank[:, 0:P], 1.0, None, ALU.max))
                    own_step(dve.reciprocal(inverse[:, :], inverse[:, :]))
                    own_step(dve.tensor_scalar(has_edge[:, :], degree_bank[:, P:P + 1], 1.0, None, ALU.min))
                    dve.scalar_tensor_tensor(result[:, :], s.bias[:, :], has_edge[:, :], own[:, :], ALU.mult, ALU.add)
                    for f in range(FC):
                        last = dve.tensor_tensor(mean[:, f, :], mean_bank[:, f * P:(f + 1) * P], inverse[:, :], ALU.mult)
                    own_step(last)
                    own_step(dve.scalar_tensor_tensor(mean[:, :, :], h_bank.rearrange("p (f n) -> p f n", f=FC), -SCALE,
                                                      mean[:, :, :], ALU.mult, ALU.add))
                    own_step(dve.tensor_copy(turned[:, 1, 0], mean[:, :, :]))
                    dve.tensor_tensor(turned[:, 1, 1], mean[:, :, :], turned[:, 1, 0], ALU.subtract)\
                        .then_inc(mean_split, 1)
                    dve.wait_ge(out_ready, tiles.value() + 1)
                    dve.scalar_tensor_tensor(result[:, :], out_bank[:, :], fold[:, :], result[:, :],
                                             ALU.mult, ALU.add).then_inc(result_done, 1)
                    tiles.add()

                dve.wait_ge(set_up, 3)
                tile_by_tile(dve, own_part, chunk_part, tile_part)

            @block.tensor
            def _(pe):
                items, tiles = Count(pe, "pe_items"), Count(pe, "pe_tiles")
                pe.wait_ge(set_up, 3)

                def own_part(t):
                    pe.wait_ge(item_ready, items.value() + 1)
                    for f in range(FC):
                        last = pe.transpose(h_bank[:, f * P:(f + 1) * P], h[:, f * P:(f + 1) * P], ident[:, :])
                    pe.matmul(mean_bank[:, :], zeros[:, 0:P], zeros[:, :], start=True, stop=False,
                              skip_group_check=True)
                    last = pe.matmul(degree_bank[:, 0:P + 1], zeros[:, 0:P], zeros[:, 0:P + 1], start=True, stop=False,
                                     skip_group_check=True)
                    last.then_inc(item_used, 1)
                    items.add()

                def chunk_part(chunk):
                    pe.wait_ge(item_ready, items.value() + 1)
                    for f in range(FC):
                        c = slice(f * P, (f + 1) * P)
                        for part in (h_hi, h_lo):
                            pe.matmul(mean_bank[:, c], part[:, c], to_node[:, :], start=False, stop=False,
                                      skip_group_check=True)
                    pe.matmul(degree_bank[:, 0:P], ones16[:, :], to_node[:, :], start=False, stop=False,
                              skip_group_check=True)
                    pe.matmul(degree_bank[:, P:P + 1], to_node[:, :], ones16[:, 0:1], start=False, stop=False,
                              skip_group_check=True).then_inc(item_used, 1)
                    items.add()

                def tile_part(t):
                    pe.wait_ge(mean_split, tiles.value() + 1)
                    for k in range(2):
                        for f in range(FC):
                            for hi_lo, part in ((0, 0), (0, 1), (1, 0)):
                                last = pe.matmul(out_bank[:, :], turned[:, k, hi_lo, f, :], weights[:, k, part, f, :],
                                                 start=(k == f == hi_lo == part == 0),
                                                 stop=(k == 1 and f == FC - 1 and hi_lo == 1))
                    last.then_inc(out_ready, 1)
                    tiles.add()

                tile_by_tile(pe, own_part, chunk_part, tile_part)


_INS = ["x", "src", "dst", "L0_gnn_W_l", "L0_gnn_b_l", "L0_gnn_W_r"]


def kernel(**inputs):
    import numpy as _np
    import concourse.bacc as _bacc
    from concourse import mybir as _mybir
    from concourse.bass_utils import run_bass_kernel_spmd as _run

    nc = _bacc.Bacc("TRN2", target_bir_lowering=False, num_devices=1)
    arrays, args = {}, []
    for name in _INS:
        a = _np.ascontiguousarray(inputs[name])
        arrays[f"in_{name}_dram"] = a
        args.append(nc.dram_tensor(f"in_{name}_dram", a.shape, _mybir.dt.from_np(a.dtype), kind="ExternalInput").ap())
    shape = arrays["in_x_dram"].shape
    out = nc.dram_tensor("out_0_dram", shape, _mybir.dt.float32, kind="ExternalOutput").ap()
    gnn_kernel(nc, *args, out)
    r = _run(nc, [arrays], core_ids=[0])
    return r.results[0]["out_0_dram"]
```
